# Optimizing a Trainium2 kernel written in Bass

```python
import numpy as np
import jax
import jax.numpy as jnp

def _softmax(x, axis=-1):
    return jax.nn.softmax(x, axis=axis)

def _gelu(x):
    return jax.nn.gelu(x, approximate=True)

def _silu(x):
    return jax.nn.silu(x)

def _sigmoid(x):
    return jax.nn.sigmoid(x)

def _layernorm(x, axis=-1, eps=1e-05):
    m = jnp.mean(x, axis=axis, keepdims=True)
    v = jnp.var(x, axis=axis, keepdims=True)
    return (x - m) / jnp.sqrt(v + eps)

def _scatter_add(tgt, idx, src, axis=0):
    return tgt.at[idx].add(src)

def _segment_sum(src, seg, n):
    return jax.ops.segment_sum(src, seg, n)
kernel_name = 'mk_vit_tower_d1_tok_img1024_r4_9b05f6'

def setup_inputs(seed: int=0):
    np.random.seed(seed)
    _w = jnp.asarray

    def _rec_inputs():
        import jax
        import jax.numpy as jnp
        _rk = jax.random.key(seed)
        x = -0.00016672 + 0.999947 * jax.random.normal(jax.random.fold_in(_rk, 1), (32, 3, 96, 96), jnp.float32)
        return x
    x = _rec_inputs()

    def _L0_tok_setup():
        import jax, jax.numpy as jnp
        import numpy as np
        EMBED_DIM = 256
        IMAGE_SIZE = 96
        CHANNELS = 3
        PATCH = 16
        NUM_PATCHES = (IMAGE_SIZE // PATCH) ** 2
        PATCH_DIM = PATCH * PATCH * CHANNELS

        def _patchify(x, patch):
            B, C, H, W = x.shape
            hp, wp = (H // patch, W // patch)
            x = x.reshape(B, C, hp, patch, wp, patch)
            x = x.transpose(0, 2, 4, 1, 3, 5)
            return x.reshape(B, hp * wp, C * patch * patch)
        key = jax.random.key(seed)
        k_x, k_w, k_b, k_cls, k_pos = jax.random.split(key, 5)
        x = jax.random.normal(k_x, (64, CHANNELS, IMAGE_SIZE, IMAGE_SIZE), dtype=jnp.float32)
        W = jax.random.normal(k_w, (EMBED_DIM, PATCH_DIM), dtype=jnp.float32) / np.sqrt(PATCH_DIM)
        b = jax.random.normal(k_b, (EMBED_DIM,), dtype=jnp.float32) * 0.01
        cls_token = jax.random.normal(k_cls, (1, 1, EMBED_DIM), dtype=jnp.float32)
        pos_embedding = jax.random.normal(k_pos, (1, 1 + NUM_PATCHES, EMBED_DIM), dtype=jnp.float32)
        return {'x': x, 'W': W, 'b': b, 'cls_token': cls_token, 'pos_embedding': pos_embedding}
    _L0_tok_all = _L0_tok_setup()
    _L0_tok_in = {k: v for k, v in _L0_tok_all.items() if k in ('W', 'b', 'cls_token', 'pos_embedding')}
    del _L0_tok_all

    def _L0_attn_setup():
        import jax, jax.numpy as jnp
        import numpy as np
        import math
        H = 16
        N_EMBD = 256
        EPS = 1e-05
        key = jax.random.key(seed)
        ks = jax.random.split(key, 6)
        B, T, C = (2, 512, 256)
        x = jax.random.normal(ks[0], (B, T, C), dtype=jnp.float32)
        s = 0.02
        Wq = jax.random.normal(ks[1], (C, N_EMBD), dtype=jnp.float32) * s
        Wk = jax.random.normal(ks[2], (C, N_EMBD), dtype=jnp.float32) * s
        Wv = jax.random.normal(ks[3], (C, N_EMBD), dtype=jnp.float32) * s
        Wo = jax.random.normal(ks[4], (N_EMBD, C), dtype=jnp.float32) * s
        return {'x': x, 'Wq': Wq, 'bq': jnp.zeros((N_EMBD,), jnp.float32), 'Wk': Wk, 'bk': jnp.zeros((N_EMBD,), jnp.float32), 'Wv': Wv, 'bv': jnp.zeros((N_EMBD,), jnp.float32), 'Wo': Wo, 'bo': jnp.zeros((C,), jnp.float32), 'gamma': jnp.ones((C,), jnp.float32), 'beta': jnp.zeros((C,), jnp.float32)}
    _L0_attn_all = _L0_attn_setup()
    _L0_attn_in = {k: v for k, v in _L0_attn_all.items() if k in ('Wq', 'bq', 'Wk', 'bk', 'Wv', 'bv', 'Wo', 'bo', 'gamma', 'beta')}
    del _L0_attn_all

    def _L0_ffn_setup():
        import jax, jax.numpy as jnp
        import numpy as np
        B, S, D = (4, 512, 256)
        E, F = (8, 1024)
        key = jax.random.key(seed)
        ks = jax.random.split(key, 5)
        x = jax.random.normal(ks[0], (B, S, D), dtype=jnp.float32)
        switch_w = jax.random.normal(ks[1], (D, E), dtype=jnp.float32) * D ** (-0.5)
        switch_b = jnp.zeros((E,), dtype=jnp.float32)
        w1 = jax.random.normal(ks[2], (E, D, F), dtype=jnp.float32) * D ** (-0.5)
        b1 = jnp.zeros((E, F), dtype=jnp.float32)
        w2 = jax.random.normal(ks[3], (E, F, D), dtype=jnp.float32) * F ** (-0.5)
        b2 = jnp.zeros((E, D), dtype=jnp.float32)
        return {'x': x, 'switch_w': switch_w, 'switch_b': switch_b, 'w1': w1, 'b1': b1, 'w2': w2, 'b2': b2}
    _L0_ffn_all = _L0_ffn_setup()
    _L0_ffn_in = {k: v for k, v in _L0_ffn_all.items() if k in ('switch_w', 'switch_b', 'w1', 'b1', 'w2', 'b2')}
    del _L0_ffn_all
    return {'x': x, 'L0_tok_W': _L0_tok_in['W'], 'L0_tok_b': _L0_tok_in['b'], 'L0_tok_cls_token': _L0_tok_in['cls_token'], 'L0_tok_pos_embedding': _L0_tok_in['pos_embedding'], 'L0_attn_Wq': _L0_attn_in['Wq'], 'L0_attn_bq': _L0_attn_in['bq'], 'L0_attn_Wk': _L0_attn_in['Wk'], 'L0_attn_bk': _L0_attn_in['bk'], 'L0_attn_Wv': _L0_attn_in['Wv'], 'L0_attn_bv': _L0_attn_in['bv'], 'L0_attn_Wo': _L0_attn_in['Wo'], 'L0_attn_bo': _L0_attn_in['bo'], 'L0_attn_gamma': _L0_attn_in['gamma'], 'L0_attn_beta': _L0_attn_in['beta'], 'L0_ffn_switch_w': _L0_ffn_in['switch_w'], 'L0_ffn_switch_b': _L0_ffn_in['switch_b'], 'L0_ffn_w1': _L0_ffn_in['w1'], 'L0_ffn_b1': _L0_ffn_in['b1'], 'L0_ffn_w2': _L0_ffn_in['w2'], 'L0_ffn_b2': _L0_ffn_in['b2']}

def reference(x, L0_tok_W, L0_tok_b, L0_tok_cls_token, L0_tok_pos_embedding, L0_attn_Wq, L0_attn_bq, L0_attn_Wk, L0_attn_bk, L0_attn_Wv, L0_attn_bv, L0_attn_Wo, L0_attn_bo, L0_attn_gamma, L0_attn_beta, L0_ffn_switch_w, L0_ffn_switch_b, L0_ffn_w1, L0_ffn_b1, L0_ffn_w2, L0_ffn_b2):
    import jax
    import jax.numpy as jnp

    def _L0_tok_ref(x, W, b, cls_token, pos_embedding):
        import jax, jax.numpy as jnp
        import numpy as np
        EMBED_DIM = 256
        IMAGE_SIZE = 96
        CHANNELS = 3
        PATCH = 16
        NUM_PATCHES = (IMAGE_SIZE // PATCH) ** 2
        PATCH_DIM = PATCH * PATCH * CHANNELS

        def _patchify(x, patch):
            B, C, H, W = x.shape
            hp, wp = (H // patch, W // patch)
            x = x.reshape(B, C, hp, patch, wp, patch)
            x = x.transpose(0, 2, 4, 1, 3, 5)
            return x.reshape(B, hp * wp, C * patch * patch)
        B = x.shape[0]
        patches = _patchify(x, PATCH)
        tokens = jnp.einsum('bnd,ed->bne', patches, W) + b
        cls = jnp.broadcast_to(cls_token, (B, 1, EMBED_DIM))
        out = jnp.concatenate([cls, tokens], axis=1)
        return out + pos_embedding

    def _L0_attn_ref(x, Wq, bq, Wk, bk, Wv, bv, Wo, bo, gamma, beta):
        import jax, jax.numpy as jnp
        import numpy as np
        import math
        H = 16
        N_EMBD = 256
        EPS = 1e-05
        B, T, _ = x.shape
        Dh = N_EMBD // H

        def split_heads(y):
            return y.reshape(B, T, H, Dh).transpose(0, 2, 1, 3)
        q = split_heads(x @ Wq + bq)
        k = split_heads(x @ Wk + bk)
        v = split_heads(x @ Wv + bv)
        att = jnp.einsum('bhtd,bhsd->bhts', q, k) * (1.0 / math.sqrt(Dh))
        causal = jnp.tril(jnp.ones((T, T), dtype=bool))
        att = jnp.where(causal[None, None], att, -jnp.inf)
        att = jax.nn.softmax(att, axis=-1)
        o = jnp.einsum('bhts,bhsd->bhtd', att, v)
        o = o.transpose(0, 2, 1, 3).reshape(B, T, N_EMBD)
        y = o @ Wo + bo
        mu = jnp.mean(y, axis=-1, keepdims=True)
        var = jnp.var(y, axis=-1, keepdims=True)
        return (y - mu) * jax.lax.rsqrt(var + EPS) * gamma + beta

    def _L0_ffn_ref(x, switch_w, switch_b, w1, b1, w2, b2):
        import jax, jax.numpy as jnp
        import numpy as np
        B, S, D = (4, 512, 256)
        E, F = (8, 1024)
        b, s, d = x.shape
        t = x.reshape(-1, d)
        logits = t @ switch_w + switch_b
        route_prob = jax.nn.softmax(logits, axis=-1)
        route_prob_max = jnp.max(route_prob, axis=-1)
        routes = jnp.argmax(route_prob, axis=-1)
        out = jnp.zeros_like(t)
        n_experts = w1.shape[0]
        for e in range(n_experts):
            h = jax.nn.gelu(t @ w1[e] + b1[e])
            y = h @ w2[e] + b2[e]
            mask = (routes == e)[:, None]
            out = jnp.where(mask, y, out)
        out = out * route_prob_max[:, None]
        return out.reshape(b, s, d)
    h = _L0_tok_ref(x, L0_tok_W, L0_tok_b, L0_tok_cls_token, L0_tok_pos_embedding)
    h = h + _L0_attn_ref(_layernorm(h, axis=-1), L0_attn_Wq, L0_attn_bq, L0_attn_Wk, L0_attn_bk, L0_attn_Wv, L0_attn_bv, L0_attn_Wo, L0_attn_bo, L0_attn_gamma, L0_attn_beta)
    h = h + _L0_ffn_ref(_layernorm(h, axis=-1), L0_ffn_switch_w, L0_ffn_switch_b, L0_ffn_w1, L0_ffn_b1, L0_ffn_w2, L0_ffn_b2)
    return h

_drawn_inputs = setup_inputs


def setup_inputs(seed=0):
    import zlib

    import numpy as np

    out = dict(_drawn_inputs(seed))
    spreads = {'L0_attn_bq': (0.0, 0.726),
     'L0_attn_bk': (0.0, 0.8),
     'L0_attn_bv': (0.0, 0.1),
     'L0_attn_bo': (0.0, 0.1),
     'L0_attn_gamma': (1.0, 0.2),
     'L0_attn_beta': (0.0, 0.1),
     'L0_ffn_switch_b': (0.0, 0.1),
     'L0_ffn_b1': (0.0, 0.549),
     'L0_ffn_b2': (0.0, 0.38)}
    factors = {'L0_tok_b': 4.752}
    for name, (base, spread) in spreads.items():
        noise = np.random.default_rng([zlib.crc32(name.encode()), seed]).standard_normal(out[name].shape)
        drawn = base * np.exp(spread * noise) if base else spread * noise
        out[name] = jnp.asarray(drawn.astype(out[name].dtype))
    for name, factor in factors.items():
        out[name] = (out[name] * factor).astype(out[name].dtype)
    return out
```

```python
import numpy as np
import concourse.bass as bass
from concourse import mybir
from contextlib import ExitStack

IMAGES, EMBED, PATCH, SIDE, CHANNELS = 32, 256, 16, 96, 3
GRID = SIDE // PATCH
TOKENS = GRID * GRID + 1
PIXELS = CHANNELS * PATCH * PATCH
PER = 3
GROUPS = -(-IMAGES // PER)
T = PER * TOKENS
ROWS = IMAGES * TOKENS
HEADS, HEAD = 16, 16
EXPERTS, HIDDEN = 8, 1024
P = 128
KP, KE, KH = PIXELS // P, EMBED // P, HIDDEN // P
BLOCKS = (ROWS + (P - 1) * EXPERTS) // P
REGION = ROWS
PAY = 2 * EMBED + 2
RING = 4
IN_FLIGHT = 6
VALUES = HEADS * (HEAD + 1)
EPS = 1e-5
MASKED = -1e30
THRESH = -(-ROWS // P)

TABLE = {}


def _columns():
    at = 0
    for name, n in (("even", 1), ("odd", 1), ("trash_out", 1), ("row", 1), ("descending", EXPERTS),
                    ("first_slot", EXPERTS), ("valid", GROUPS), ("trash_slot", GROUPS), ("token", GROUPS),
                    ("block", BLOCKS), ("threshold", EXPERTS * THRESH), ("upto", EXPERTS * EXPERTS),
                    ("expert", EXPERTS)):
        TABLE[name] = (at, at + n)
        at += n
    return at


TABLE_N = _columns()


def vit_layer(nc, patches, w_embed, position, first_row, w_qk, b_qk, w_v, w_o, rows4, w_switch, b_switch,
              b1, b2, experts, table, identity, masks, no_ids, out):
    f32, bf16, i32 = mybir.dt.float32, mybir.dt.bfloat16, mybir.dt.int32
    ALU, ACT, AX = mybir.AluOpType, mybir.ActivationFunctionType, mybir.AxisListType
    SCALE = float(HEAD) ** -0.5
    ds = bass.ds

    ctx = ExitStack()
    with ctx:
        def sb(name, cols, dt=f32, parts=P):
            return ctx.enter_context(nc.sbuf_tensor(name, [parts, cols], dt))

        def sem(name):
            return ctx.enter_context(nc.semaphore(name))

        W = sb("expert_weights", EXPERTS * 2 * KE * HIDDEN)
        W2_AT = EXPERTS * KE * HIDDEN
        tab = sb("table_sb", TABLE_N)
        ident = sb("ident", P)
        b1_sb = sb("b1_sb", EXPERTS * KH)
        b2_sb = sb("b2_sb", EXPERTS * EMBED)
        expert_of = sb("expert_of", BLOCKS, i32)
        source_rows = sb("source_rows", BLOCKS, i32)
        live = sb("live", BLOCKS)

        front = sb("front", KP * EMBED + KP * T)
        w_embed_sb, patch_sb = front[:, 0:KP * EMBED], front[:, KP * EMBED:KP * (EMBED + T)]
        gathered_rows = [front[:, i * PAY:(i + 1) * PAY] for i in range(RING)]
        position_sb = sb("position_sb", EMBED)
        first_row_sb = sb("first_row_sb", EMBED)
        w_qk_sb = sb("w_qk_sb", KE * 2 * EMBED)
        b_qk_sb = sb("b_qk_sb", 4)
        w_v_sb = sb("w_v_sb", KE * EMBED)
        w_o_sb = sb("w_o_sb", KE * EMBED)
        rows4_sb = sb("rows4_sb", 4 * EMBED)
        bv, bo, gamma, beta = (rows4_sb[0:T, i * EMBED:(i + 1) * EMBED] for i in range(4))
        w_switch_sb = sb("w_switch_sb", KE * EXPERTS)
        b_switch_sb = sb("b_switch_sb", EXPERTS)
        masks_sb = sb("masks_sb", 4 * T + T + P + T, bf16)
        causal, earlier = masks_sb[0:T, 0:4 * T], masks_sb[0:T, 4 * T:5 * T]
        ones_b, ident_b = masks_sb[0:T, 5 * T:5 * T + P], masks_sb[0:T, 5 * T + P:6 * T + P]

        hidden = sb("hidden", IN_FLIGHT * EMBED)
        normed = sb("normed", EMBED)
        normedT = sb("normedT", KE * T)
        qT = sb("qT", KE * T)
        kT = [sb("kT_even", KE * T), sb("kT_odd", KE * T)]
        values = sb("values", 2 * VALUES)
        big = sb("big", 2 * HEADS * T)
        probs, probsT = big[:, 0:HEADS * T], big[:, HEADS * T:2 * HEADS * T]
        weighted = sb("weighted", EMBED)
        weightedT = sb("weightedT", KE * T)
        attn = sb("attn", EMBED)
        attn_g = sb("attn_g", EMBED)
        payload = sb("payload", PAY)
        normed2T = sb("normed2T", KE * T)
        stats = sb("stats", 18)
        moments = sb("moments", 6)
        var_eps = sb("var_eps", 3)
        rstd = sb("rstd", 3)
        newton = sb("newton", 6)
        best_score = sb("best_score", HEADS)
        top = sb("top", HEADS)
        inv = sb("inv", HEADS)
        logits = sb("logits", EXPERTS)
        best = sb("best", 4)
        shifted = sb("shifted", EXPERTS)
        numer = sb("numer", EXPERTS)
        picks = sb("picks", EXPERTS)
        onehot = sb("onehot", EXPERTS, bf16)
        rank = sb("rank", EXPERTS)
        rank_own = sb("rank_own", EXPERTS)
        next_slot = sb("next_slot", EXPERTS)
        slot_f = sb("slot_f", 1)
        slot = sb("slot", 1, i32)
        token_now = sb("token_now", 1, i32)

        xT = sb("xT", KE * P)
        h1, hT = big[:, 0:HIDDEN], big[:, HIDDEN:2 * HIDDEN]
        result = [big[:, 2 * HIDDEN + i * EMBED:2 * HIDDEN + (i + 1) * EMBED] for i in range(RING)]
        ffn_sum = sb("ffn_sum", EMBED)
        source_now = sb("source_now", RING, i32)
        token_of = sb("token_of", RING, i32)
        target_f = sb("target_f", 1)
        target = sb("target", RING, i32)
        scratch = sb("scratch", BLOCKS * EXPERTS)
        of_block = sb("of_block", BLOCKS * EXPERTS)
        t8 = sb("t8", 4 * EXPERTS)
        t17 = sb("t17", 6 * BLOCKS)

        bank = [ctx.enter_context(nc.psum_tensor(f"bank{i}", [P, 512], f32)) for i in range(8)]
        scores = bank[0:4]
        p_k, p_v = bank[4][:, 0:KE * T], bank[4][0:T, KE * T:KE * T + EMBED]
        p_q, p_nT = bank[5][:, 0:KE * T], bank[5][:, KE * T:2 * KE * T]
        p_h, p_n2T = bank[6][0:T, 0:EMBED], bank[6][:, EMBED:EMBED + KE * T]
        p_logits = bank[6][0:T, 480:488]
        p_rank, p_count = bank[6][0:T, 488:496], bank[6][:, 496:504]
        p_o, p_wT = bank[7][0:T, 0:HEADS * (HEAD + 1)], bank[7][:, 0:KE * T]
        p_y = bank[7][0:T, EMBED:2 * EMBED]
        p_h1, p_hT, p_ffn, p_xT = bank[0:2], bank[2:4], bank[4], bank[5]

        def col(name, parts=P, at=None):
            a, b = TABLE[name]
            if at is None:
                return tab[0:parts, a:b]
            return tab[0:parts, ds(a + at, 1)]

        embed_loaded, attn_loaded, ffn_loaded = sem("embed_loaded"), sem("attn_loaded"), sem("ffn_loaded")
        patches_loaded, embedded, hidden_made = sem("patches_loaded"), sem("embedded"), sem("hidden_made")
        dve_ready = sem("dve_ready")
        a_stats, a_moments = sem("a_stats"), sem("a_moments")
        rstd_steps, normed_made = sem("rstd_steps"), sem("normed_made")
        normed_turned, normedT_made = sem("normed_turned"), sem("normedT_made")
        q_made, v_made, q_copied, k_copied, v_copied = (
            sem("q_made"), sem("v_made"), sem("q_copied"), sem("k_copied"), sem("v_copied"))
        scored, top_found, probs_made = sem("scored"), sem("top_found"), sem("probs_made")
        probs_turned, probsT_act, probsT_dve = sem("probs_turned"), sem("probsT_act"), sem("probsT_dve")
        summed, inverted, weighted_made = sem("summed"), sem("inverted"), sem("weighted_made")
        weighted_turned, weightedT_made = sem("weighted_turned"), sem("weightedT_made")
        projected, attn_made, c_stats, c_moments, attn_g_made = (
            sem("projected"), sem("attn_made"), sem("c_stats"), sem("c_moments"), sem("attn_g_made"))
        beta_added, residual_made, d_stats, d_moments = (
            sem("beta_added"), sem("residual_made"), sem("d_stats"), sem("d_moments"))
        normed2_made, normed2_turned, normed2T_made = (
            sem("normed2_made"), sem("normed2_turned"), sem("normed2T_made"))
        logits_made, route_steps, numer_made = sem("logits_made"), sem("route_steps"), sem("numer_made")
        ranked, payload_copied = sem("ranked"), sem("payload_copied")
        ids_cleared, token_set, ids_scattered, rows_written = (
            sem("ids_cleared"), sem("token_set"), sem("ids_scattered"), sem("rows_written"))
        tables_steps = sem("tables_steps")
        source_set = sem("source_set")
        ids_gathered, gathered = (
            [sem(f"{name}_{r}") for r in range(RING)] for name in ("ids_gathered", "gathered"))
        stored = sem("stored")
        x_turned, xT_made, ffn_hidden, h1_copied, h_turned, gelu_made = (
            sem("x_turned"), sem("xT_made"), sem("ffn_hidden"), sem("h1_copied"), sem("h_turned"),
            sem("gelu_made"))
        ffn_done, ffn_read, target_diff, target_made, result_made = (
            sem("ffn_done"), sem("ffn_read"), sem("target_diff"), sem("target_made"), sem("result_made"))
        prob_made = sem("prob_made")
        sp_passed, pool_passed, dve_passed = sem("sp_passed"), sem("pool_passed"), sem("dve_passed")
        own_rank, top_read = sem("own_rank"), sem("top_read")
        rows_dram = nc.dram_tensor("rows_dram", (GROUPS * T, PAY), f32).ap()
        ids_dram = nc.dram_tensor("ids_dram", (EXPERTS * REGION + P, 1), i32).ap()

        EMBED_LOADS, ATTN_LOADS = 5, 9
        WEIGHT_LOADS = 16
        RSTD_STEPS, ROUTE_STEPS = 12, 7
        TABLE_STEPS = 23
        LAST = GROUPS + 4
        FULL = 5
        STEADY = RING + 1
        TURNS = (BLOCKS - 2 - STEADY) // RING

        def hidden_of(g):
            return hidden[0:T, ds(g % IN_FLIGHT * EMBED, EMBED)]

        def head_of(n):
            r, j = n // 4, n % 4
            return j // 2 * (P // HEAD) + 2 * r + j % 2

        def runs(t, stage):
            return not isinstance(t, int) or 0 <= t - stage < GROUPS

        def later(g, n=1):
            return not isinstance(g, int) or g >= n

        def steps(eng, step):
            for t in range(FULL):
                step(t)
            with eng.Fori(FULL, GROUPS) as t:
                step(t)
            for t in range(GROUPS, LAST):
                step(t)

        def block_steps(eng, step):
            for b in range(-1, STEADY):
                step(b, b % RING)
            with eng.Fori(0, TURNS) as turn:
                for i in range(RING):
                    step(turn * RING + STEADY + i, (STEADY + i) % RING)
            for b in range(STEADY + TURNS * RING, BLOCKS + 1):
                step(b, b % RING)

        def turns(b):
            return 16 * (b // RING) + 16

        def inside(b):
            return not isinstance(b, int) or 0 <= b < BLOCKS

        block = ctx.enter_context(nc.Block())

        @block.sync
        def _(sp):
            sp.dma_start(w_embed_sb, w_embed).then_inc(embed_loaded, 16)
            sp.dma_start(patch_sb, patches[0, :, :]).then_inc(patches_loaded, 16)
            sp.dma_start(position_sb[0:T, :], position).then_inc(embed_loaded, 16)
            sp.dma_start(first_row_sb[0:T, :], first_row).then_inc(embed_loaded, 16)
            sp.dma_start(ident[:, :], identity).then_inc(embed_loaded, 16)
            sp.dma_start(tab[:, :], table).then_inc(embed_loaded, 16)
            for dst, src in ((w_qk_sb, w_qk), (b_qk_sb, b_qk), (w_v_sb, w_v), (rows4_sb, rows4),
                             (w_o_sb, w_o), (w_switch_sb, w_switch), (b_switch_sb, b_switch)):
                sp.dma_start(dst[:, :], src).then_inc(attn_loaded, 16)
            sp.dma_start(big[0:T, 0:masks_sb.shape[1]], masks).then_inc(attn_loaded, 16)
            sp.dma_start(b1_sb[:, :], b1).then_inc(attn_loaded, 16)

            sp.dma_start(ids_dram, no_ids).then_inc(ids_cleared, 16)
            sp.dma_start(b2_sb[:, :], b2).then_inc(ffn_loaded, 16)

            def load_patches(g):
                sp.wait_ge(embedded, g)
                sp.dma_start(patch_sb, patches[ds(g, 1), :, :].rearrange("a p n -> (a p) n")) \
                    .then_inc(patches_loaded, 16)

            each = W.shape[1] // WEIGHT_LOADS
            early = WEIGHT_LOADS - (GROUPS - FULL)

            def load_weights(n):
                sp.dma_start(W[:, ds(n * each, each)], experts[:, ds(n * each, each)]).then_inc(ffn_loaded, 16)

            def write_rows(g):
                sp.wait_ge(payload_copied, 2 * g + 2)
                sp.sem_inc(sp_passed)
                sp.wait_ge(prob_made, g + 1)
                sp.wait_ge(normed2_made, g + 1)
                sp.dma_start(rows_dram[ds(g * T, T), :], payload[0:T, :]).then_inc(rows_written, 16)

            def step(t):
                if runs(t + 1, 0):
                    load_patches(t + 1)
                if not isinstance(t, int):
                    load_weights(early + t - FULL)
                elif 1 <= t < FULL:
                    for n in range(early * (t - 1) // (FULL - 1), early * t // (FULL - 1)):
                        load_weights(n)
                if runs(t, 4):
                    write_rows(t - 4)

            for t in range(FULL):
                step(t)
            with sp.Fori(FULL, GROUPS - 1) as t:
                step(t)
            load_weights(WEIGHT_LOADS - 1)
            for t in range(GROUPS - 1, LAST):
                step(t)

        @block.gpsimd
        def _(pool):
            def settled():
                pool.sem_inc(pool_passed)

            def add_beta(g):
                pool.wait_ge(normed_made, g + 1)
                settled()
                h = hidden_of(g)
                nc.gpsimd.tensor_tensor(h, h, beta, ALU.add).then_inc(beta_added, 1)

            def fill_payload(g):
                if later(g):
                    pool.wait_ge(rows_written, 16 * g)
                pool.wait_ge(d_stats, g + 1)
                settled()
                nc.gpsimd.tensor_copy(payload[0:T, 0:EMBED], hidden_of(g)).then_inc(payload_copied, 1)
                nc.gpsimd.tensor_copy(payload[0:T, PAY - 1:PAY], col("token", T, g)).then_inc(payload_copied, 1)

            def scatter_ids(g):
                if later(g):
                    pool.wait_ge(ids_scattered, 16 * g)
                    settled()
                nc.gpsimd.tensor_copy(token_now[0:T, :], col("token", T, g)).then_inc(token_set, 1)
                pool.wait_ge(token_set, g + 1)
                settled()
                pool.wait_ge(route_steps, ROUTE_STEPS * g + ROUTE_STEPS)
                settled()
                nc.gpsimd.indirect_dma_start(ids_dram[:, :], bass.IndirectOffsetOnAxis(slot[0:T, 0:1], 0),
                                             token_now[0:T, :], None).then_inc(ids_scattered, 16)

            def step(t):
                if runs(t, 4):
                    fill_payload(t - 4)
                if runs(t, 1):
                    add_beta(t - 1)
                if runs(t, 4):
                    scatter_ids(t - 4)

            pool.wait_ge(embed_loaded, 16 * EMBED_LOADS)
            pool.wait_ge(attn_loaded, 16 * ATTN_LOADS)
            pool.wait_ge(ids_cleared, 16)
            steps(pool, step)

            def find(b, r):
                if later(b, RING):
                    pool.wait_ge(gathered[r], turns(b - RING))
                    settled()
                nc.gpsimd.tensor_copy(source_now[:, r:r + 1], source_rows[:, ds(b, 1)]).then_inc(source_set, 1)
                pool.wait_ge(source_set, b + 1)
                settled()
                nc.gpsimd.indirect_dma_start(token_of[:, r:r + 1], None, ids_dram[:, :],
                                             bass.IndirectOffsetOnAxis(source_now[:, r:r + 1], 0)) \
                    .then_inc(ids_gathered[r], 16)

            def fetch(b, r):
                if later(b, RING):
                    pool.wait_ge(result_made, b - RING + 1)
                    settled()
                pool.wait_ge(ids_gathered[r], turns(b))
                settled()
                nc.gpsimd.indirect_dma_start(gathered_rows[r], None, rows_dram[:, :],
                                             bass.IndirectOffsetOnAxis(token_of[:, r:r + 1], 0)) \
                    .then_inc(gathered[r], 16)

            def store(b, r):
                if later(b):
                    pool.wait_ge(stored, 16 * b)
                    settled()
                pool.wait_ge(target_made, b + 1)
                settled()
                pool.wait_ge(result_made, b + 1)
                settled()
                nc.gpsimd.indirect_dma_start(out[:, :], bass.IndirectOffsetOnAxis(target[:, r:r + 1], 0),
                                             result[r], None).then_inc(stored, 16)

            pool.wait_ge(ids_scattered, 16 * GROUPS)
            pool.wait_ge(tables_steps, TABLE_STEPS)
            find(0, 0)
            find(1, 1)
            pool.wait_ge(rows_written, 16 * GROUPS)
            fetch(0, 0)

            def block_step(b, r):
                if inside(b + 3):
                    find(b + 3, (r + 3) % RING)
                if inside(b + 2):
                    fetch(b + 2, (r + 2) % RING)
                if inside(b - 1):
                    store(b - 1, (r - 1) % RING)

            block_steps(pool, block_step)
            pool.wait_ge(stored, 16 * BLOCKS)

        @block.scalar
        def _(act):
            def copy_q(g):
                act.wait_ge(q_made, g + 1)
                if later(g):
                    act.wait_ge(scored, g)
                for c in range(KE):
                    ins = nc.scalar.activation(qT[:, c * T:(c + 1) * T], p_q[:, c * T:(c + 1) * T],
                                               ACT.Identity, bias=b_qk_sb[:, c:c + 1])
                ins.then_inc(q_copied, 1)

            def copy_probsT(g):
                if later(g):
                    act.wait_ge(summed, g)
                for r in (0, 1):
                    act.wait_ge(probs_turned, 4 * g + r + 1)
                    nc.scalar.activation(probsT[0:T, r * 4 * T:(r + 1) * 4 * T], scores[r][0:T, 0:4 * T],
                                         ACT.Copy).then_inc(probsT_act, 1)

            def softmax(g, rs):
                if rs[0] == 0 and later(g):
                    act.wait_ge(probs_turned, 4 * g)
                act.wait_ge(top_found, 2 * g + 1 + rs[0] // 2)
                for r in rs:
                    for j in range(4):
                        n = 4 * r + j
                        ins = nc.scalar.activation(probs[0:T, n * T:(n + 1) * T], scores[r][0:T, j * T:(j + 1) * T],
                                                   ACT.Exp, bias=top[0:T, n:n + 1], scale=SCALE)
                    ins.then_inc(probs_made, 1)

            def copy_normedT(g):
                act.wait_ge(normed_turned, g + 1)
                if later(g):
                    act.wait_ge(v_made, g)
                nc.scalar.activation(normedT[:, :], p_nT, ACT.Copy).then_inc(normedT_made, 1)

            def copy_normed2T(g):
                act.wait_ge(normed2_turned, g + 1)
                if later(g):
                    act.wait_ge(logits_made, g)
                nc.scalar.activation(normed2T[:, :], p_n2T, ACT.Copy).then_inc(normed2T_made, 1)

            def copy_weightedT(g):
                act.wait_ge(weighted_turned, g + 1)
                if later(g):
                    act.wait_ge(projected, g)
                nc.scalar.activation(weightedT[:, :], p_wT, ACT.Copy).then_inc(weightedT_made, 1)

            def route_numer(g):
                act.wait_ge(route_steps, ROUTE_STEPS * g + 3)
                if later(g):
                    act.wait_ge(route_steps, ROUTE_STEPS * g)
                nc.scalar.activation(numer[0:T, :], shifted[0:T, :], ACT.Exp,
                                     accum_out=best[0:T, 2:3]).then_inc(numer_made, 1)

            def step(t):
                if runs(t, 1):
                    copy_q(t - 1)
                if runs(t, 2):
                    copy_probsT(t - 2)
                if runs(t, 4):
                    copy_normed2T(t - 4)
                if runs(t, 0):
                    copy_normedT(t)
                if runs(t, 1):
                    softmax(t - 1, (0, 1))
                if runs(t, 2):
                    copy_weightedT(t - 2)
                if runs(t, 4):
                    route_numer(t - 4)
                if runs(t, 1):
                    softmax(t - 1, (2, 3))

            act.wait_ge(attn_loaded, 16 * ATTN_LOADS)
            act.wait_ge(dve_ready, 5)
            steps(act, step)

            act.wait_ge(tables_steps, TABLE_STEPS)

            def block_step(b, r):
                if inside(b + 1):
                    act.wait_ge(x_turned, b + 2)
                    if later(b, 0):
                        act.wait_ge(ffn_hidden, 2 * b + 2)
                    nc.scalar.activation(xT[:, :], p_xT[:, 0:KE * P], ACT.Copy).then_inc(xT_made, 1)
                if inside(b):
                    e = act.value_load(expert_of[0:1, ds(b, 1)], min_val=0, max_val=EXPERTS - 1)
                    if later(b):
                        act.wait_ge(ffn_done, b)
                    for f in range(KH):
                        if f % 4 == 0:
                            act.wait_ge(h_turned, 2 * b + 1 + f // 4)
                        ins = nc.scalar.activation(hT[:, f * P:(f + 1) * P],
                                                   p_hT[f // 4][:, f % 4 * P:(f % 4 + 1) * P],
                                                   ACT.Gelu_apprx_tanh, bias=b1_sb[:, ds(e * KH + f, 1)])
                    ins.then_inc(gelu_made, 1)

            block_steps(act, block_step)

        @block.tensor
        def _(pe):
            mm, turn = nc.tensor.matmul, nc.tensor.transpose

            def embed(g):
                pe.wait_ge(patches_loaded, 16 * g + 16)
                if later(g):
                    pe.wait_ge(hidden_made, g)
                if later(g, 5):
                    pe.wait_ge(route_steps, ROUTE_STEPS * (g - 4))
                for k in range(KP):
                    ins = mm(p_h, patch_sb[:, k * T:(k + 1) * T], w_embed_sb[:, k * EMBED:(k + 1) * EMBED],
                             start=(k == 0), stop=(k == KP - 1))
                ins.then_inc(embedded, 1)

            def turn_normed(g):
                pe.wait_ge(normed_made, g + 1)
                if later(g):
                    pe.wait_ge(normedT_made, g)
                for c in range(KE):
                    ins = turn(p_nT[:, c * T:(c + 1) * T], normed[0:T, c * P:(c + 1) * P], ident[0:T, 0:T])
                ins.then_inc(normed_turned, 1)

            def project_qkv(g):
                pe.wait_ge(normedT_made, g + 1)
                if later(g):
                    pe.wait_ge(q_copied, g)
                for c in range(4):
                    if c == 2 and later(g):
                        pe.wait_ge(v_copied, g)
                    for k in range(KE):
                        ins = mm((p_q if c < 2 else p_k)[:, c % 2 * T:(c % 2 + 1) * T],
                                 w_qk_sb[:, (k * 4 + c) * P:(k * 4 + c + 1) * P],
                                 normedT[:, k * T:(k + 1) * T], start=(k == 0), stop=(k == KE - 1))
                    if c == 1:
                        ins.then_inc(q_made, 1)
                for k in range(KE):
                    ins = mm(p_v, normedT[:, k * T:(k + 1) * T], w_v_sb[:, k * EMBED:(k + 1) * EMBED],
                             start=(k == 0), stop=(k == KE - 1))
                ins.then_inc(v_made, 1)

            def score(g):
                if later(g):
                    pe.wait_ge(probsT_act, 2 * g)
                    pe.wait_ge(probsT_dve, 2 * g)
                for r in range(4):
                    mm(scores[r][0:T, 0:4 * T], ident_b, causal, start=True, stop=False, skip_group_check=True)
                pe.wait_ge(q_copied, g + 1)
                pe.wait_ge(k_copied, g + 1)
                for j in range(4):
                    c, parity = j // 2, j % 2
                    for r in range(4):
                        ins = mm(scores[r][0:T, j * T:(j + 1) * T],
                                 qT[32 * r:32 * r + 32, c * T:(c + 1) * T],
                                 kT[parity][32 * r:32 * r + 32, c * T:(c + 1) * T],
                                 start=False, stop=True, skip_group_check=True)
                ins.then_inc(scored, 1)

            def turn_probs(g):
                for r in range(4):
                    pe.wait_ge(probs_made, 4 * g + r + 1)
                    for j in range(4):
                        n = 4 * r + j
                        ins = turn(scores[r][0:T, j * T:(j + 1) * T], probs[0:T, n * T:(n + 1) * T],
                                   ident[0:T, 0:T])
                    ins.then_inc(probs_turned, 1)

            def weigh_values(g):
                pe.wait_ge(probsT_act, 2 * g + 2)
                pe.wait_ge(probsT_dve, 2 * g + 2)
                pe.wait_ge(v_copied, g + 1)
                if later(g):
                    pe.wait_ge(attn_made, g)
                for n in range(HEADS):
                    h = head_of(n)
                    ins = mm(p_o[:, h * (HEAD + 1):(h + 1) * (HEAD + 1)], probsT[0:T, n * T:(n + 1) * T],
                             values[0:T, ds(g % 2 * VALUES + h * (HEAD + 1), HEAD + 1)], start=True, stop=True)
                ins.then_inc(summed, 1)

            def turn_weighted(g):
                pe.wait_ge(weighted_made, g + 1)
                for c in range(KE):
                    ins = turn(p_wT[:, c * T:(c + 1) * T], weighted[0:T, c * P:(c + 1) * P], ident[0:T, 0:T])
                ins.then_inc(weighted_turned, 1)

            def project_out(g):
                pe.wait_ge(weightedT_made, g + 1)
                for k in range(KE):
                    ins = mm(p_y, weightedT[:, k * T:(k + 1) * T], w_o_sb[:, k * EMBED:(k + 1) * EMBED],
                             start=(k == 0), stop=(k == KE - 1))
                ins.then_inc(projected, 1)

            def after(g):
                return g + 5 if not isinstance(g, int) else min(g + 5, GROUPS)

            def turn_normed2(g):
                pe.wait_ge(normed2_made, g + 1)
                pe.wait_ge(hidden_made, after(g))
                for c in range(KE):
                    ins = turn(p_n2T[:, c * T:(c + 1) * T], payload[0:T, EMBED + c * P:EMBED + (c + 1) * P],
                               ident[0:T, 0:T])
                ins.then_inc(normed2_turned, 1)

            def route(g):
                pe.wait_ge(normed2T_made, g + 1)
                for k in range(KE):
                    ins = mm(p_logits, normed2T[:, k * T:(k + 1) * T], w_switch_sb[:, k * EXPERTS:(k + 1) * EXPERTS],
                             start=(k == 0), stop=(k == KE - 1))
                ins.then_inc(logits_made, 1)

            def count(g):
                pe.wait_ge(route_steps, ROUTE_STEPS * g + 6)
                mm(p_rank, earlier, onehot[0:T, :], start=True, stop=True)
                mm(p_count, ones_b, onehot[0:T, :], start=True, stop=True).then_inc(ranked, 1)

            def step(t):
                if runs(t, 1):
                    project_qkv(t - 1)
                if runs(t, 2):
                    turn_probs(t - 2)
                if runs(t, 0):
                    embed(t)
                if runs(t, 1):
                    score(t - 1)
                if runs(t, 0):
                    turn_normed(t)
                if runs(t, 4):
                    turn_normed2(t - 4)
                if runs(t, 2):
                    weigh_values(t - 2)
                if runs(t, 4):
                    route(t - 4)
                if runs(t, 2):
                    turn_weighted(t - 2)
                if runs(t, 4):
                    count(t - 4)
                if runs(t, 2):
                    project_out(t - 2)

            pe.wait_ge(embed_loaded, 16 * EMBED_LOADS)
            pe.wait_ge(attn_loaded, 16 * ATTN_LOADS)
            pe.wait_ge(dve_ready, 5)
            steps(pe, step)

            pe.wait_ge(ffn_loaded, 16 * (WEIGHT_LOADS + 1))
            pe.wait_ge(tables_steps, TABLE_STEPS)

            def block_step(b, r):
                if inside(b + 1):
                    pe.wait_ge(gathered[(r + 1) % RING], turns(b + 1))
                    if later(b, 0):
                        pe.wait_ge(xT_made, b + 1)
                    rows = gathered_rows[(r + 1) % RING]
                    for c in range(KE):
                        ins = turn(p_xT[:, c * P:(c + 1) * P], rows[:, EMBED + c * P:EMBED + (c + 1) * P],
                                   ident[:, :])
                    ins.then_inc(x_turned, 1)
                if inside(b - 1):
                    e = pe.value_load(expert_of[0:1, ds(b - 1, 1)], min_val=0, max_val=EXPERTS - 1)
                    pe.wait_ge(gelu_made, b)
                    if later(b - 1):
                        pe.wait_ge(ffn_read, b - 1)
                    for f in range(KH):
                        ins = mm(p_ffn[:, 0:EMBED], hT[:, f * P:(f + 1) * P],
                                 W[:, ds(W2_AT + e * KH * EMBED + f * EMBED, EMBED)],
                                 start=(f == 0), stop=(f == KH - 1))
                    ins.then_inc(ffn_done, 1)
                if inside(b):
                    for f in range(KH):
                        if f % 4 == 0:
                            pe.wait_ge(h1_copied, 2 * b + 1 + f // 4)
                        ins = turn(p_hT[f // 4][:, f % 4 * P:(f % 4 + 1) * P], h1[:, f * P:(f + 1) * P], ident[:, :])
                        if f % 4 == 3:
                            ins.then_inc(h_turned, 1)
                if inside(b + 1):
                    e = pe.value_load(expert_of[0:1, ds(b + 1, 1)], min_val=0, max_val=EXPERTS - 1)
                    pe.wait_ge(xT_made, b + 2)
                    for half in range(2):
                        for k in range(KE):
                            ins = mm(p_h1[half][:, :], xT[:, k * P:(k + 1) * P],
                                     W[:, ds(e * KE * HIDDEN + k * HIDDEN + half * 512, 512)],
                                     start=(k == 0), stop=(k == KE - 1))
                        ins.then_inc(ffn_hidden, 1)

            block_steps(pe, block_step)

        @block.vector
        def _(dve):
            v = nc.vector

            def settled():
                dve.sem_inc(dve_passed)

            def mean(i):
                return moments[0:T, 2 * i:2 * i + 1]

            def layer_stats(i, rows, made, g, stats_sem, moments_sem):
                dve.wait_ge(made, g + 1)
                settled()
                v.bn_stats(stats[0:T, 6 * i:6 * i + 6], rows).then_inc(stats_sem, 1)
                dve.wait_ge(stats_sem, g + 1)
                settled()
                v.bn_aggr(moments[0:T, 2 * i:2 * i + 2], stats[0:T, 6 * i:6 * i + 6]).then_inc(moments_sem, 1)

            def copy_k(g):
                dve.wait_ge(v_made, g + 1)
                if later(g):
                    dve.wait_ge(scored, g)
                for c in range(KE):
                    for parity, name in enumerate(("even", "odd")):
                        ins = v.tensor_scalar(kT[parity][:, c * T:(c + 1) * T], p_k[:, c * T:(c + 1) * T],
                                              b_qk_sb[:, 2 + c:3 + c], col(name), ALU.add, ALU.mult)
                ins.then_inc(k_copied, 1)

            def copy_probsT(g):
                if later(g):
                    dve.wait_ge(summed, g)
                for r in (2, 3):
                    dve.wait_ge(probs_turned, 4 * g + r + 1)
                    v.tensor_copy(probsT[0:T, r * 4 * T:(r + 1) * 4 * T], scores[r][0:T, 0:4 * T]) \
                        .then_inc(probsT_dve, 1)

            def embed_rows(g):
                dve.wait_ge(embedded, g + 1)
                v.tensor_tensor(hidden_of(g), p_h, position_sb[0:T, :], ALU.add) \
                    .then_inc(hidden_made, 1)
                layer_stats(0, hidden_of(g), hidden_made, g, a_stats, a_moments)

            def inverse_deviations(t):
                for stage, moments_sem in ((0, a_moments), (3, c_moments), (4, d_moments)):
                    if runs(t, stage):
                        dve.wait_ge(moments_sem, t - stage + 1)
                n = [RSTD_STEPS * t]

                def link(ins):
                    n[0] = n[0] + 1
                    ins.then_inc(rstd_steps, 1)
                    dve.wait_ge(rstd_steps, n[0])

                square, factor = newton[0:T, 0:3], newton[0:T, 3:6]
                x, y = var_eps[0:T, :], rstd[0:T, :]
                variance = moments[0:T, :].rearrange("p (i c) -> p i c", c=2)[:, :, 1]
                link(v.tensor_scalar(x, variance, EPS, None, ALU.add))
                link(v.tensor_scalar(square.bitcast(i32), x.bitcast(i32), 1, None, ALU.logical_shift_right))
                link(v.tensor_scalar(y.bitcast(i32), square.bitcast(i32), -1.0, float(0x5F3759DF),
                                     ALU.mult, ALU.add))
                for _ in range(3):
                    link(v.tensor_tensor(square, y, y, ALU.mult))
                    link(v.scalar_tensor_tensor(square, square, -0.5, x, ALU.mult, ALU.mult))
                    link(v.scalar_tensor_tensor(y, square, 1.5, y, ALU.add, ALU.mult))

            def normalize(g):
                if later(g):
                    dve.wait_ge(normed_turned, g)
                v.tensor_scalar(normed[0:T, :], hidden_of(g), mean(0), rstd[0:T, 0:1],
                                ALU.subtract, ALU.mult).then_inc(normed_made, 1)

            def normalize2(g):
                if later(g):
                    dve.wait_ge(rows_written, 16 * g)
                    dve.wait_ge(normed2_turned, g)
                v.tensor_scalar(payload[0:T, EMBED:2 * EMBED], hidden_of(g), mean(2),
                                rstd[0:T, 2:3], ALU.subtract, ALU.mult).then_inc(normed2_made, 1)

            def add_residual(g):
                dve.wait_ge(beta_added, g + 1)
                dve.wait_ge(attn_g_made, g + 1)
                h = hidden_of(g)
                v.scalar_tensor_tensor(h, attn_g[0:T, :], rstd[0:T, 1:2], h, ALU.mult, ALU.add) \
                    .then_inc(residual_made, 1)
                layer_stats(2, h, residual_made, g, d_stats, d_moments)

            def find_top(g):
                if later(g):
                    dve.wait_ge(probs_made, 4 * g)
                dve.wait_ge(scored, g + 1)
                for half in range(2):
                    for r in (2 * half, 2 * half + 1):
                        ins = v.tensor_reduce(best_score[0:T, 4 * r:4 * r + 4],
                                              scores[r][0:T, 0:4 * T].rearrange("p (j s) -> p j s", s=T),
                                              AX.X, ALU.max)
                        ins.then_inc(top_read, 1)
                    dve.wait_ge(top_read, 4 * g + 2 * half + 2)
                    v.tensor_scalar(top[0:T, 8 * half:8 * half + 8], best_score[0:T, 8 * half:8 * half + 8],
                                    -SCALE, None, ALU.mult).then_inc(top_found, 1)

            def copy_values(g):
                v.tensor_tensor(values[0:T, ds(g % 2 * VALUES, VALUES)].rearrange("p (h d) -> p h d", h=HEADS)[:, :, 0:HEAD],
                                p_v.rearrange("p (h d) -> p h d", h=HEADS),
                                bv.rearrange("p (h d) -> p h d", h=HEADS), ALU.add).then_inc(v_copied, 1)

            def divide(g):
                o = p_o.rearrange("p (h d) -> p h d", h=HEADS)
                dve.wait_ge(summed, g + 1)
                v.reciprocal(inv[0:T, :], o[:, :, HEAD]).then_inc(inverted, 1)
                dve.wait_ge(inverted, g + 1)
                if later(g):
                    dve.wait_ge(weighted_turned, g)
                v.tensor_tensor(weighted[0:T, :].rearrange("p (h d) -> p h d", h=HEADS), o[:, :, 0:HEAD],
                                inv[0:T, :].unsqueeze(2).broadcast_to([T, HEADS, HEAD]), ALU.mult) \
                    .then_inc(weighted_made, 1)

            def attention_rows(g):
                dve.wait_ge(projected, g + 1)
                v.tensor_tensor(attn[0:T, :], p_y, bo, ALU.add).then_inc(attn_made, 1)
                layer_stats(1, attn[0:T, :], attn_made, g, c_stats, c_moments)
                dve.wait_ge(c_moments, g + 1)
                v.scalar_tensor_tensor(attn_g[0:T, :], attn[0:T, :], mean(1), gamma, ALU.subtract, ALU.mult) \
                    .then_inc(attn_g_made, 1)

            def pick(g):
                n = ROUTE_STEPS * g
                z = shifted[0:T, :]
                dve.wait_ge(logits_made, g + 1)
                v.tensor_tensor(logits[0:T, :], p_logits, b_switch_sb[0:T, :], ALU.add).then_inc(route_steps, 1)
                dve.wait_ge(route_steps, n + 1)
                v.tensor_reduce(best[0:T, 0:1], logits[0:T, :], AX.X, ALU.max).then_inc(route_steps, 1)
                dve.wait_ge(route_steps, n + 2)
                if later(g):
                    dve.wait_ge(numer_made, g)
                v.tensor_scalar(z, logits[0:T, :], best[0:T, 0:1], None, ALU.subtract).then_inc(route_steps, 1)
                dve.wait_ge(route_steps, n + 3)
                v.scalar_tensor_tensor(picks[0:T, :], z, 0.0, col("descending", T), ALU.is_equal, ALU.mult) \
                    .then_inc(route_steps, 1)
                dve.wait_ge(route_steps, n + 4)
                v.tensor_reduce(best[0:T, 1:2], picks[0:T, :], AX.X, ALU.max).then_inc(route_steps, 1)
                dve.wait_ge(route_steps, n + 5)
                if later(g):
                    dve.wait_ge(ranked, g)
                v.tensor_scalar(onehot[0:T, :], picks[0:T, :], best[0:T, 1:2], col("valid", T, g),
                                ALU.is_equal, ALU.mult).then_inc(route_steps, 1)

            def place(g):
                dve.wait_ge(numer_made, g + 1)
                v.reciprocal(payload[0:T, 2 * EMBED:2 * EMBED + 1], best[0:T, 2:3]).then_inc(prob_made, 1)
                dve.wait_ge(ranked, g + 1)
                if later(g):
                    dve.wait_ge(own_rank, 4 * g)
                v.tensor_tensor(rank[0:T, :], p_rank, next_slot[0:T, :], ALU.add).then_inc(own_rank, 1)
                dve.wait_ge(own_rank, 4 * g + 1)
                v.tensor_tensor(rank_own[0:T, :], rank[0:T, :], onehot[0:T, :], ALU.mult).then_inc(own_rank, 1)
                dve.wait_ge(own_rank, 4 * g + 2)
                v.tensor_reduce(slot_f[0:T, :], rank_own[0:T, :], AX.X, ALU.add).then_inc(own_rank, 1)
                v.tensor_tensor(next_slot[:, :], p_count, next_slot[:, :], ALU.add).then_inc(own_rank, 1)
                dve.wait_ge(own_rank, 4 * g + 3)
                if later(g):
                    dve.wait_ge(ids_scattered, 16 * g)
                v.tensor_tensor(slot[0:T, :], slot_f[0:T, :], col("trash_slot", T, g), ALU.add) \
                    .then_inc(route_steps, 1)

            def step(t):
                if runs(t, 1):
                    copy_k(t - 1)
                    copy_values(t - 1)
                if runs(t, 2):
                    copy_probsT(t - 2)
                if runs(t, 0):
                    embed_rows(t)
                inverse_deviations(t)
                if runs(t, 4):
                    normalize2(t - 4)
                if runs(t, 0):
                    normalize(t)
                if runs(t, 1):
                    find_top(t - 1)
                if runs(t, 2):
                    divide(t - 2)
                if runs(t, 4):
                    pick(t - 4)
                if runs(t, 3):
                    add_residual(t - 3)
                if runs(t, 4):
                    place(t - 4)
                if runs(t, 2):
                    attention_rows(t - 2)

            v.memset(moments[:, :], 1.0).then_inc(dve_ready, 1)
            v.memset(values[:, :], 1.0).then_inc(dve_ready, 1)
            dve.wait_ge(dve_ready, 2)
            dve.wait_ge(embed_loaded, 16 * EMBED_LOADS)
            v.tensor_copy(next_slot[:, :], col("first_slot")).then_inc(dve_ready, 1)
            v.tensor_tensor(position_sb[0:T, :], position_sb[0:T, :], first_row_sb[0:T, :], ALU.add) \
                .then_inc(dve_ready, 1)
            dve.wait_ge(attn_loaded, 16 * ATTN_LOADS)
            v.tensor_copy(masks_sb[0:T, :], big[0:T, 0:masks_sb.shape[1]]).then_inc(dve_ready, 1)
            dve.wait_ge(dve_ready, 5)
            steps(dve, step)

            n = [0]

            def link(ins):
                n[0] += 1
                ins.then_inc(tables_steps, 1)
                dve.wait_ge(tables_steps, n[0])

            def cube(ap, mid, last):
                return ap.rearrange("p (a b) -> p a b", b=last)

            def over(ap, mid, last):
                return ap.unsqueeze(2).broadcast_to([P, mid, last])

            def each_row(ap, mid, last):
                return ap.unsqueeze(1).broadcast_to([P, mid, last])

            E, B = EXPERTS, BLOCKS
            counts, needs, ends, starts = (t8[:, i * E:(i + 1) * E] for i in range(4))
            number, own, start_of, count_of, last_of, at = (t17[:, i * B:(i + 1) * B] for i in range(6))
            wide = scratch[:, 0:E * THRESH]
            dve.wait_ge(own_rank, 4 * GROUPS)
            link(v.tensor_tensor(counts, next_slot[:, :], col("first_slot"), ALU.subtract))
            link(v.tensor_tensor(cube(wide, E, THRESH), over(counts, E, THRESH),
                                 cube(col("threshold"), E, THRESH), ALU.is_gt))
            link(v.tensor_reduce(needs, cube(wide, E, THRESH), AX.X, ALU.add))
            square = scratch[:, 0:E * E]
            link(v.tensor_tensor(cube(square, E, E), each_row(needs, E, E), cube(col("upto"), E, E), ALU.mult))
            link(v.tensor_reduce(ends, cube(square, E, E), AX.X, ALU.add))
            link(v.tensor_tensor(starts, ends, needs, ALU.subtract))
            link(v.tensor_scalar(best[:, 3:4], ends[:, E - 1:E], -1.0, None, ALU.add))
            link(v.tensor_scalar(number, col("block"), best[:, 3:4], None, ALU.min))
            link(v.tensor_tensor(cube(scratch[:, :], B, E), each_row(ends, B, E), over(number, B, E), ALU.is_le))
            link(v.tensor_reduce(own, cube(scratch[:, :], B, E), AX.X, ALU.add))
            link(v.tensor_copy(expert_of[:, :], own))
            link(v.tensor_tensor(cube(of_block[:, :], B, E), over(own, B, E), each_row(col("expert"), B, E),
                                 ALU.is_equal))
            link(v.tensor_tensor(cube(scratch[:, :], B, E), cube(of_block[:, :], B, E), each_row(starts, B, E),
                                 ALU.mult))
            link(v.tensor_reduce(start_of, cube(scratch[:, :], B, E), AX.X, ALU.add))
            link(v.tensor_tensor(cube(scratch[:, :], B, E), cube(of_block[:, :], B, E), each_row(counts, B, E),
                                 ALU.mult))
            link(v.tensor_reduce(count_of, cube(scratch[:, :], B, E), AX.X, ALU.add))
            link(v.tensor_tensor(at, number, start_of, ALU.subtract))
            link(v.tensor_scalar(at, at, float(P), col("row"), ALU.mult, ALU.add))
            link(v.tensor_scalar(last_of, count_of, -1.0, None, ALU.add))
            link(v.tensor_tensor(last_of, at, last_of, ALU.min))
            link(v.scalar_tensor_tensor(source_rows[:, :], own, float(REGION), last_of, ALU.mult, ALU.add))
            link(v.tensor_tensor(at, at, count_of, ALU.is_lt))
            link(v.scalar_tensor_tensor(live[:, :], col("block"), ends[:, E - 1:E], at, ALU.is_lt, ALU.mult))
            assert n[0] == TABLE_STEPS

            def block_step(b, r):
                if inside(b):
                    if later(b):
                        dve.wait_ge(h_turned, 2 * b)
                    for half in range(2):
                        dve.wait_ge(ffn_hidden, 2 * b + half + 1)
                        v.tensor_copy(h1[:, half * 512:(half + 1) * 512], p_h1[half][:, :]).then_inc(h1_copied, 1)
                if inside(b - 1):
                    q = (r - 1) % RING
                    rows = gathered_rows[q]
                    e = dve.value_load(expert_of[0:1, ds(b - 1, 1)], min_val=0, max_val=EXPERTS - 1)
                    dve.wait_ge(ffn_done, b)
                    if later(b - 1):
                        dve.wait_ge(result_made, b - 1)
                        dve.wait_ge(target_made, b - 1)
                    v.tensor_tensor(ffn_sum[:, :], p_ffn[:, 0:EMBED], b2_sb[:, ds(e * EMBED, EMBED)], ALU.add) \
                        .then_inc(ffn_read, 1)
                    if later(b - 1, RING):
                        dve.wait_ge(stored, 16 * (b - RING))
                    v.scalar_tensor_tensor(target_f[:, :], rows[:, PAY - 1:PAY], col("trash_out"),
                                           live[:, ds(b - 1, 1)], ALU.subtract, ALU.mult).then_inc(target_diff, 1)
                    dve.wait_ge(target_diff, b)
                    v.tensor_tensor(target[:, q:q + 1], target_f[:, :], col("trash_out"), ALU.add) \
                        .then_inc(target_made, 1)
                    dve.wait_ge(ffn_read, b)
                    v.scalar_tensor_tensor(result[q], ffn_sum[:, :], rows[:, PAY - 2:PAY - 1], rows[:, 0:EMBED],
                                           ALU.mult, ALU.add).then_inc(result_made, 1)

            block_steps(dve, block_step)


def _constants():
    tab = np.zeros((P, TABLE_N), np.float32)
    row = np.arange(P)

    def put(name, value):
        a, b = TABLE[name]
        tab[:, a:b] = value

    put("even", (row % 32 < 16)[:, None])
    put("odd", (row % 32 >= 16)[:, None])
    put("trash_out", (ROWS + row)[:, None])
    put("row", row[:, None])
    put("descending", EXPERTS - np.arange(EXPERTS))
    put("first_slot", REGION * np.arange(EXPERTS))
    token = T * np.arange(GROUPS)[None, :] + row[:, None]
    put("valid", token < ROWS)
    put("trash_slot", (token >= ROWS) * (EXPERTS * REGION + row[:, None]))
    put("token", token)
    put("block", np.arange(BLOCKS))
    put("threshold", np.tile(P * np.arange(THRESH), EXPERTS))
    e = np.arange(EXPERTS)
    put("upto", (e[None, :] <= e[:, None]).reshape(-1))
    put("expert", e)
    t = np.arange(T)
    seen = (t[:, None] // TOKENS == t[None, :] // TOKENS) & (t[None, :] <= t[:, None])
    masks = np.concatenate([np.tile(np.where(seen, 0.0, MASKED), (1, 4)), t[:, None] < t[None, :],
                            np.ones((T, P)), np.eye(T)], axis=1).astype(np.float32)
    return tab, np.eye(P, dtype=np.float32), masks


def kernel(**inputs):
    import concourse.bacc as _bacc
    from concourse.bass_utils import run_bass_kernel_spmd as _run

    x = {k: np.asarray(a) for k, a in inputs.items()}

    def rows_first(w, k):
        return w.reshape(k, P, -1).transpose(1, 0, 2).reshape(P, -1)

    def everywhere(v, parts=P):
        return np.broadcast_to(v.reshape(1, -1), (parts, v.size))

    img = x["x"].reshape(IMAGES, CHANNELS, GRID, PATCH, GRID, PATCH).transpose(1, 3, 5, 0, 2, 4)
    filled = np.zeros((PIXELS, GROUPS * PER, TOKENS), np.float32)
    filled[:, :IMAGES, 1:] = img.reshape(PIXELS, IMAGES, TOKENS - 1)
    patches = filled.reshape(KP, P, GROUPS, T).transpose(2, 1, 0, 3).reshape(GROUPS, P, KP * T)
    first = np.concatenate([x["L0_tok_cls_token"].reshape(1, EMBED),
                            everywhere(x["L0_tok_b"], TOKENS - 1)])
    w_qk = np.concatenate([x["L0_attn_Wq"], x["L0_attn_Wk"]], axis=1)
    b_qk = np.concatenate([x["L0_attn_bq"], x["L0_attn_bk"]]).reshape(4, P).T
    w1 = x["L0_ffn_w1"].reshape(EXPERTS, KE, P, HIDDEN).transpose(2, 0, 1, 3).reshape(P, -1)
    w2 = x["L0_ffn_w2"].reshape(EXPERTS, KH, P, EMBED).transpose(2, 0, 1, 3).reshape(P, -1)
    tab, eye, masks = _constants()
    arrays = {
        "patches": patches,
        "w_embed": rows_first(x["L0_tok_W"].T, KP),
        "position": np.tile(x["L0_tok_pos_embedding"].reshape(TOKENS, EMBED), (PER, 1)),
        "first_row": np.tile(first, (PER, 1)),
        "w_qk": rows_first(w_qk, KE), "b_qk": b_qk,
        "w_v": rows_first(x["L0_attn_Wv"], KE), "w_o": rows_first(x["L0_attn_Wo"], KE),
        "rows4": everywhere(np.concatenate([x["L0_attn_bv"], x["L0_attn_bo"], x["L0_attn_gamma"],
                                            x["L0_attn_beta"]])),
        "w_switch": rows_first(x["L0_ffn_switch_w"], KE), "b_switch": everywhere(x["L0_ffn_switch_b"]),
        "b1": x["L0_ffn_b1"].reshape(EXPERTS * KH, P).T, "b2": everywhere(x["L0_ffn_b2"]),
        "experts": np.concatenate([w1, w2], axis=1),
        "table": tab, "identity": eye, "masks": masks,
        "no_ids": np.zeros((EXPERTS * REGION + P, 1), np.int32),
    }
    nc = _bacc.Bacc("TRN2", target_bir_lowering=False, num_devices=1)
    arrays = {k: np.ascontiguousarray(a) for k, a in arrays.items()}
    args = [nc.dram_tensor(f"in_{k}_dram", a.shape, mybir.dt.from_np(a.dtype), kind="ExternalInput").ap()
            for k, a in arrays.items()]
    out = nc.dram_tensor("out_0_dram", (ROWS + P, EMBED), mybir.dt.float32, kind="ExternalOutput").ap()
    vit_layer(nc, *args, out)
    r = _run(nc, [{f"in_{k}_dram": a for k, a in arrays.items()}], core_ids=[0])
    return r.results[0]["out_0_dram"][:ROWS].reshape(IMAGES, TOKENS, EMBED)
```

```python
import numpy as np
import concourse.bass as bass
from concourse import mybir
from contextlib import ExitStack

IMAGES, EMBED, PATCH, SIDE, CHANNELS = 32, 256, 16, 96, 3
GRID = SIDE // PATCH
TOKENS = GRID * GRID + 1
PIXELS = CHANNELS * PATCH * PATCH
PER = 3
GROUPS = -(-IMAGES // PER)
T = PER * TOKENS
ROWS = IMAGES * TOKENS
HEADS, HEAD = 16, 16
EXPERTS, HIDDEN = 8, 1024
P = 128
KP, KE, KH = PIXELS // P, EMBED // P, HIDDEN // P
BLOCKS = (ROWS + (P - 1) * EXPERTS) // P
REGION = ROWS
PAY = 2 * EMBED + 2
RING = 4
IN_FLIGHT = 6
VALUES = 2 * HEADS * HEAD
EPS = 1e-5
MASKED = -1e30
THRESH = -(-ROWS // P)

TABLE = {}


def _columns():
    at = 0
    for name, n in (("even", 1), ("odd", 1), ("trash_out", 1), ("row", 1), ("descending", EXPERTS),
                    ("first_slot", EXPERTS), ("valid", GROUPS), ("trash_slot", GROUPS), ("token", GROUPS),
                    ("block", BLOCKS), ("threshold", EXPERTS * THRESH), ("upto", EXPERTS * EXPERTS),
                    ("expert", EXPERTS)):
        TABLE[name] = (at, at + n)
        at += n
    return at


TABLE_N = _columns()


def vit_layer(nc, patches, w_embed, position, first_row, w_qk, b_qk, w_v, w_o, rows4, w_switch, b_switch,
              b1, b2, experts, table, identity, masks, no_ids, out):
    f32, bf16, i32 = mybir.dt.float32, mybir.dt.bfloat16, mybir.dt.int32
    ALU, ACT, AX = mybir.AluOpType, mybir.ActivationFunctionType, mybir.AxisListType
    SCALE = float(HEAD) ** -0.5
    ds = bass.ds

    ctx = ExitStack()
    with ctx:
        def sb(name, cols, dt=f32, parts=P):
            return ctx.enter_context(nc.sbuf_tensor(name, [parts, cols], dt))

        def sem(name):
            return ctx.enter_context(nc.semaphore(name))

        W = sb("expert_weights", EXPERTS * 2 * KE * HIDDEN)
        W2_AT = EXPERTS * KE * HIDDEN
        tab = sb("table_sb", TABLE_N)
        ident = sb("ident", P)
        b1_sb = sb("b1_sb", EXPERTS * KH)
        b2_sb = sb("b2_sb", EXPERTS * EMBED)
        expert_of = sb("expert_of", BLOCKS, i32)
        source_rows = sb("source_rows", BLOCKS, i32)
        live = sb("live", BLOCKS)

        front = sb("front", KP * EMBED + KP * T)
        w_embed_sb, patch_sb = front[:, 0:KP * EMBED], front[:, KP * EMBED:KP * (EMBED + T)]
        gathered_rows = [front[:, i * PAY:(i + 1) * PAY] for i in range(RING)]
        position_sb = sb("position_sb", EMBED)
        first_row_sb = sb("first_row_sb", EMBED)
        w_qk_sb = sb("w_qk_sb", KE * 2 * EMBED)
        b_qk_sb = sb("b_qk_sb", 4)
        k_bias = sb("k_bias", 2 * KE)
        w_v_sb = sb("w_v_sb", KE * EMBED)
        w_o_sb = sb("w_o_sb", KE * EMBED)
        rows4_sb = sb("rows4_sb", 4 * EMBED)
        bv, bo, gamma, beta = (rows4_sb[0:T, i * EMBED:(i + 1) * EMBED] for i in range(4))
        w_switch_sb = sb("w_switch_sb", KE * EXPERTS)
        b_switch_sb = sb("b_switch_sb", EXPERTS)
        masks_sb = sb("masks_sb", 4 * T + T + P + T, bf16)
        causal, earlier = masks_sb[0:T, 0:4 * T], masks_sb[0:T, 4 * T:5 * T]
        ones_b, ident_b = masks_sb[0:T, 5 * T:5 * T + P], masks_sb[0:T, 5 * T + P:6 * T + P]

        hidden = sb("hidden", IN_FLIGHT * EMBED)
        normed = sb("normed", EMBED)
        normedT = sb("normedT", KE * T)
        qT = sb("qT", KE * T)
        kT = [sb("kT_even", KE * T), sb("kT_odd", KE * T)]
        values = [sb(f"values_{i}", VALUES) for i in range(2)]
        big = sb("big", 2 * HEADS * T)
        probs, probsT = big[:, 0:HEADS * T], big[:, HEADS * T:2 * HEADS * T]
        sums = sb("sums", HEADS)
        inverse = sb("inverse", HEADS)
        inverse_wide = sb("inverse_wide", EMBED)
        inverseT = sb("inverseT", KE * T)
        weightedT = sb("weightedT", KE * T)
        attn = sb("attn", EMBED)
        attn_g = sb("attn_g", EMBED)
        payload = sb("payload", PAY)
        normed2T = sb("normed2T", KE * T)
        stats = sb("stats", 18)
        moments = sb("moments", 6)
        var_eps = sb("var_eps", 3)
        rstd = sb("rstd", 3)
        newton = sb("newton", 6)
        best_score = sb("best_score", HEADS)
        top = sb("top", HEADS)
        logits = sb("logits", EXPERTS)
        best = sb("best", 4)
        shifted = sb("shifted", EXPERTS)
        numer = sb("numer", EXPERTS)
        picks = sb("picks", EXPERTS)
        onehot = sb("onehot", EXPERTS, bf16)
        rank = sb("rank", EXPERTS)
        rank_own = sb("rank_own", EXPERTS)
        next_slot = sb("next_slot", EXPERTS)
        slot_f = sb("slot_f", 1)
        slot = sb("slot", 1, i32)
        token_now = sb("token_now", 1, i32)

        xT = sb("xT", KE * P)
        h1, hT = big[:, 0:HIDDEN], big[:, HIDDEN:2 * HIDDEN]
        result = [big[:, 2 * HIDDEN + i * EMBED:2 * HIDDEN + (i + 1) * EMBED] for i in range(RING)]
        ffn_sum = sb("ffn_sum", EMBED)
        source_now = sb("source_now", RING, i32)
        token_of = sb("token_of", RING, i32)
        target_f = sb("target_f", 1)
        target = sb("target", RING, i32)
        scratch = sb("scratch", BLOCKS * EXPERTS)
        of_block = sb("of_block", BLOCKS * EXPERTS)
        t8 = sb("t8", 4 * EXPERTS)
        t17 = sb("t17", 6 * BLOCKS)

        bank = [ctx.enter_context(nc.psum_tensor(f"bank{i}", [P, 512], f32)) for i in range(8)]
        scores = bank[0:4]
        p_h, p_v = bank[4][0:T, 0:EMBED], bank[4][0:T, EMBED:2 * EMBED]
        p_q, p_k = bank[5][:, 0:KE * T], bank[5][:, KE * T:2 * KE * T]
        p_nT, p_n2T = bank[6][:, 0:KE * T], bank[6][:, KE * T:2 * KE * T]
        p_logits = bank[6][0:T, 480:488]
        p_rank, p_count = bank[6][0:T, 488:496], bank[6][:, 496:504]
        p_oT, p_inverseT = bank[7][:, 0:KE * T], bank[7][:, EMBED:EMBED + KE * T]
        p_y = bank[7][0:T, EMBED:2 * EMBED]
        p_h1, p_hT, p_ffn, p_xT = bank[0:2], bank[2:4], bank[4], bank[5]

        def col(name, parts=P, at=None):
            a, b = TABLE[name]
            if at is None:
                return tab[0:parts, a:b]
            return tab[0:parts, ds(a + at, 1)]

        w_embed_loaded = sem("w_embed_loaded")
        embed_loaded, attn_loaded, ffn_loaded = sem("embed_loaded"), sem("attn_loaded"), sem("ffn_loaded")
        patches_loaded, embedded, hidden_made = sem("patches_loaded"), sem("embedded"), sem("hidden_made")
        dve_ready = sem("dve_ready")
        a_stats, a_moments = sem("a_stats"), sem("a_moments")
        rstd_steps, normed_made = sem("rstd_steps"), sem("normed_made")
        normed_turned, normedT_made = sem("normed_turned"), sem("normedT_made")
        k_made, v_made, k_copied, v_copied = sem("k_made"), sem("v_made"), sem("k_copied"), sem("v_copied")
        scored, top_found, probs_made = sem("scored"), sem("top_found"), sem("probs_made")
        probs_turned, probsT_made = sem("probs_turned"), sem("probsT_made")
        inverted, inverse_made, inverse_turned, inverseT_made, weighed, weightedT_made = (
            sem("inverted"), sem("inverse_made"), sem("inverse_turned"), sem("inverseT_made"),
            sem("weighed"), sem("weightedT_made"))
        projected, attn_made, c_stats, c_moments, attn_g_made = (
            sem("projected"), sem("attn_made"), sem("c_stats"), sem("c_moments"), sem("attn_g_made"))
        beta_added, residual_made, d_stats, d_moments = (
            sem("beta_added"), sem("residual_made"), sem("d_stats"), sem("d_moments"))
        normed2_made, normed2_turned, normed2T_made = (
            sem("normed2_made"), sem("normed2_turned"), sem("normed2T_made"))
        logits_made, route_steps, numer_made = sem("logits_made"), sem("route_steps"), sem("numer_made")
        ranked, payload_copied = sem("ranked"), sem("payload_copied")
        ids_cleared, token_set, ids_scattered, rows_written = (
            sem("ids_cleared"), sem("token_set"), sem("ids_scattered"), sem("rows_written"))
        tables_steps = sem("tables_steps")
        source_set = sem("source_set")
        ids_gathered, gathered = (
            [sem(f"{name}_{r}") for r in range(RING)] for name in ("ids_gathered", "gathered"))
        stored = sem("stored")
        x_turned, xT_made, ffn_hidden, h1_copied, h_turned, gelu_made = (
            sem("x_turned"), sem("xT_made"), sem("ffn_hidden"), sem("h1_copied"), sem("h_turned"),
            sem("gelu_made"))
        ffn_done, ffn_read, target_diff, target_made, result_made = (
            sem("ffn_done"), sem("ffn_read"), sem("target_diff"), sem("target_made"), sem("result_made"))
        prob_made = sem("prob_made")
        sp_passed, pool_passed, dve_passed = sem("sp_passed"), sem("pool_passed"), sem("dve_passed")
        own_rank, top_read = sem("own_rank"), sem("top_read")
        rows_dram = nc.dram_tensor("rows_dram", (GROUPS * T, PAY), f32).ap()
        ids_dram = nc.dram_tensor("ids_dram", (EXPERTS * REGION + P, 1), i32).ap()

        EMBED_LOADS, ATTN_LOADS = 4, 9
        WEIGHT_LOADS = 16
        RSTD_STEPS, ROUTE_STEPS = 12, 7
        TABLE_STEPS = 23
        LAST = GROUPS + 4
        FULL = 5
        STEADY = RING + 1
        TURNS = (BLOCKS - 2 - STEADY) // RING

        def hidden_of(g):
            return hidden[0:T, ds(g % IN_FLIGHT * EMBED, EMBED)]

        def head_of(n):
            r, j = n // 4, n % 4
            return j // 2 * (P // HEAD) + 2 * r + j % 2

        def runs(t, stage):
            return not isinstance(t, int) or 0 <= t - stage < GROUPS

        def later(g, n=1):
            return not isinstance(g, int) or g >= n

        def steps(eng, step):
            for t in range(FULL):
                step(t, t % 2)
            with eng.Fori(0, (GROUPS - FULL) // 2) as turn:
                for i in range(2):
                    step(turn * 2 + FULL + i, (FULL + i) % 2)
            for t in range(GROUPS, LAST):
                step(t, t % 2)

        def block_steps(eng, step):
            for b in range(-1, STEADY):
                step(b, b % RING)
            with eng.Fori(0, TURNS) as turn:
                for i in range(RING):
                    step(turn * RING + STEADY + i, (STEADY + i) % RING)
            for b in range(STEADY + TURNS * RING, BLOCKS + 1):
                step(b, b % RING)

        assert (GROUPS - FULL) % 2 == 0

        def up_to(count):
            return min(count, GROUPS) if isinstance(count, int) else count

        def turns(b):
            return 16 * (b // RING) + 16

        def inside(b):
            return not isinstance(b, int) or 0 <= b < BLOCKS

        block = ctx.enter_context(nc.Block())

        @block.sync
        def _(sp):
            sp.dma_start(w_embed_sb, w_embed).then_inc(w_embed_loaded, 16)
            sp.dma_start(patch_sb, patches[0, :, :]).then_inc(patches_loaded, 16)
            sp.dma_start(position_sb[0:T, :], position).then_inc(embed_loaded, 16)
            sp.dma_start(first_row_sb[0:T, :], first_row).then_inc(embed_loaded, 16)
            sp.dma_start(ident[:, :], identity).then_inc(embed_loaded, 16)
            sp.dma_start(tab[:, :], table).then_inc(embed_loaded, 16)
            for dst, src in ((w_qk_sb, w_qk), (b_qk_sb, b_qk), (w_v_sb, w_v), (rows4_sb, rows4),
                             (w_o_sb, w_o), (w_switch_sb, w_switch), (b_switch_sb, b_switch)):
                sp.dma_start(dst[:, :], src).then_inc(attn_loaded, 16)
            sp.dma_start(big[0:T, 0:masks_sb.shape[1]], masks).then_inc(attn_loaded, 16)
            sp.dma_start(b1_sb[:, :], b1).then_inc(attn_loaded, 16)

            sp.dma_start(ids_dram, no_ids).then_inc(ids_cleared, 16)
            sp.dma_start(b2_sb[:, :], b2).then_inc(ffn_loaded, 16)

            def load_patches(g):
                sp.wait_ge(embedded, g)
                sp.dma_start(patch_sb, patches[ds(g, 1), :, :].rearrange("a p n -> (a p) n")) \
                    .then_inc(patches_loaded, 16)

            each = W.shape[1] // WEIGHT_LOADS
            early = WEIGHT_LOADS - (GROUPS - FULL)

            def load_weights(n):
                sp.dma_start(W[:, ds(n * each, each)], experts[:, ds(n * each, each)]).then_inc(ffn_loaded, 16)

            def write_rows(g):
                sp.wait_ge(payload_copied, 2 * g + 2)
                sp.sem_inc(sp_passed)
                sp.wait_ge(prob_made, g + 1)
                sp.wait_ge(normed2_made, g + 1)
                sp.dma_start(rows_dram[ds(g * T, T), :], payload[0:T, :]).then_inc(rows_written, 16)

            def step(t):
                if runs(t + 1, 0):
                    load_patches(t + 1)
                if not isinstance(t, int):
                    load_weights(early + t - FULL)
                elif 1 <= t < FULL:
                    for n in range(early * (t - 1) // (FULL - 1), early * t // (FULL - 1)):
                        load_weights(n)
                if runs(t, 4):
                    write_rows(t - 4)

            for t in range(FULL):
                step(t)
            with sp.Fori(FULL, GROUPS - 1) as t:
                step(t)
            load_weights(WEIGHT_LOADS - 1)
            for t in range(GROUPS - 1, LAST):
                step(t)

        @block.gpsimd
        def _(pool):
            def settled():
                pool.sem_inc(pool_passed)

            def add_beta(g):
                pool.wait_ge(normed_made, g + 1)
                settled()
                h = hidden_of(g)
                nc.gpsimd.tensor_tensor(h, h, beta, ALU.add).then_inc(beta_added, 1)

            def fill_payload(g):
                if later(g):
                    pool.wait_ge(rows_written, 16 * g)
                pool.wait_ge(d_stats, g + 1)
                settled()
                nc.gpsimd.tensor_copy(payload[0:T, 0:EMBED], hidden_of(g)).then_inc(payload_copied, 1)
                nc.gpsimd.tensor_copy(payload[0:T, PAY - 1:PAY], col("token", T, g)).then_inc(payload_copied, 1)

            def scatter_ids(g):
                if later(g):
                    pool.wait_ge(ids_scattered, 16 * g)
                    settled()
                nc.gpsimd.tensor_copy(token_now[0:T, :], col("token", T, g)).then_inc(token_set, 1)
                pool.wait_ge(token_set, g + 1)
                settled()
                pool.wait_ge(route_steps, ROUTE_STEPS * g + ROUTE_STEPS)
                settled()
                nc.gpsimd.indirect_dma_start(ids_dram[:, :], bass.IndirectOffsetOnAxis(slot[0:T, 0:1], 0),
                                             token_now[0:T, :], None).then_inc(ids_scattered, 16)

            def step(t, place):
                if runs(t, 4):
                    fill_payload(t - 4)
                if runs(t, 1):
                    add_beta(t - 1)
                if runs(t, 4):
                    scatter_ids(t - 4)

            pool.wait_ge(embed_loaded, 16 * EMBED_LOADS)
            pool.wait_ge(attn_loaded, 16 * ATTN_LOADS)
            pool.wait_ge(ids_cleared, 16)
            steps(pool, step)

            def find(b, r):
                if later(b, RING):
                    pool.wait_ge(gathered[r], turns(b - RING))
                    settled()
                nc.gpsimd.tensor_copy(source_now[:, r:r + 1], source_rows[:, ds(b, 1)]).then_inc(source_set, 1)
                pool.wait_ge(source_set, b + 1)
                settled()
                nc.gpsimd.indirect_dma_start(token_of[:, r:r + 1], None, ids_dram[:, :],
                                             bass.IndirectOffsetOnAxis(source_now[:, r:r + 1], 0)) \
                    .then_inc(ids_gathered[r], 16)

            def fetch(b, r):
                if later(b, RING):
                    pool.wait_ge(result_made, b - RING + 1)
                    settled()
                pool.wait_ge(ids_gathered[r], turns(b))
                settled()
                nc.gpsimd.indirect_dma_start(gathered_rows[r], None, rows_dram[:, :],
                                             bass.IndirectOffsetOnAxis(token_of[:, r:r + 1], 0)) \
                    .then_inc(gathered[r], 16)

            def store(b, r):
                if later(b):
                    pool.wait_ge(stored, 16 * b)
                    settled()
                pool.wait_ge(target_made, b + 1)
                settled()
                pool.wait_ge(result_made, b + 1)
                settled()
                nc.gpsimd.indirect_dma_start(out[:, :], bass.IndirectOffsetOnAxis(target[:, r:r + 1], 0),
                                             result[r], None).then_inc(stored, 16)

            pool.wait_ge(ids_scattered, 16 * GROUPS)
            pool.wait_ge(tables_steps, TABLE_STEPS)
            find(0, 0)
            find(1, 1)
            pool.wait_ge(rows_written, 16 * GROUPS)
            fetch(0, 0)

            def block_step(b, r):
                if inside(b + 3):
                    find(b + 3, (r + 3) % RING)
                if inside(b + 2):
                    fetch(b + 2, (r + 2) % RING)
                if inside(b - 1):
                    store(b - 1, (r - 1) % RING)

            block_steps(pool, block_step)
            pool.wait_ge(stored, 16 * BLOCKS)

        @block.scalar
        def _(act):
            def copy_q_and_k(g):
                act.wait_ge(k_made, g + 1)
                if later(g):
                    act.wait_ge(scored, 2 * g)
                for c in range(KE):
                    at = slice(c * T, (c + 1) * T)
                    nc.scalar.activation(qT[:, at], p_q[:, at], ACT.Identity, bias=b_qk_sb[:, c:c + 1])
                    for parity, name in enumerate(("even", "odd")):
                        ins = nc.scalar.activation(kT[parity][:, at], p_k[:, at], ACT.Identity,
                                                   bias=k_bias[:, KE * parity + c:KE * parity + c + 1],
                                                   scale=col(name))
                ins.then_inc(k_copied, 1)

            def copy_probsT(g):
                if later(g):
                    act.wait_ge(weighed, g)
                for r in range(4):
                    act.wait_ge(probs_turned, 4 * g + r + 1)
                    nc.scalar.activation(probsT[0:T, r * 4 * T:(r + 1) * 4 * T], scores[r][0:T, 0:4 * T],
                                         ACT.Copy).then_inc(probsT_made, 1)

            def softmax(g, rs):
                if rs[0] == 0 and later(g):
                    act.wait_ge(probs_turned, 4 * g)
                    act.wait_ge(inverted, g)
                act.wait_ge(top_found, 2 * g + 1 + rs[0] // 2)
                for r in rs:
                    for j in range(4):
                        n = 4 * r + j
                        h = head_of(n)
                        ins = nc.scalar.activation(probs[0:T, n * T:(n + 1) * T], scores[r][0:T, j * T:(j + 1) * T],
                                                   ACT.Exp, bias=top[0:T, n:n + 1], scale=SCALE,
                                                   accum_out=sums[0:T, h:h + 1])
                    ins.then_inc(probs_made, 1)

            def copy_normedT(g):
                act.wait_ge(normed_turned, g + 1)
                if runs(g, 4):
                    act.wait_ge(normed2_turned, g - 3)
                if later(g):
                    act.wait_ge(v_made, g)
                nc.scalar.activation(normedT[:, :], p_nT, ACT.Copy).then_inc(normedT_made, 1)

            def copy_normed2T(g):
                act.wait_ge(normed2_turned, g + 1)
                if later(g):
                    act.wait_ge(logits_made, g)
                nc.scalar.activation(normed2T[:, :], p_n2T, ACT.Copy).then_inc(normed2T_made, 1)

            def copy_inverseT(g):
                act.wait_ge(inverse_turned, g + 1)
                if later(g):
                    act.wait_ge(weightedT_made, g)
                nc.scalar.activation(inverseT[:, :], p_inverseT, ACT.Copy).then_inc(inverseT_made, 1)

            def route_numer(g):
                act.wait_ge(route_steps, ROUTE_STEPS * g + 3)
                if later(g):
                    act.wait_ge(route_steps, ROUTE_STEPS * g)
                nc.scalar.activation(numer[0:T, :], shifted[0:T, :], ACT.Exp,
                                     accum_out=best[0:T, 2:3]).then_inc(numer_made, 1)

            def step(t, place):
                if isinstance(t, int) and t == 1:
                    act.wait_ge(attn_loaded, 16 * ATTN_LOADS)
                    act.wait_ge(dve_ready, 7)
                if runs(t, 2):
                    copy_probsT(t - 2)
                if runs(t, 1):
                    copy_q_and_k(t - 1)
                if runs(t, 2):
                    copy_inverseT(t - 2)
                if runs(t, 0):
                    copy_normedT(t)
                if runs(t, 4):
                    copy_normed2T(t - 4)
                if runs(t, 1):
                    softmax(t - 1, (0, 1))
                if runs(t, 4):
                    route_numer(t - 4)
                if runs(t, 1):
                    softmax(t - 1, (2, 3))

            steps(act, step)

            act.wait_ge(tables_steps, TABLE_STEPS)

            def block_step(b, r):
                if inside(b + 1):
                    act.wait_ge(x_turned, b + 2)
                    if later(b, 0):
                        act.wait_ge(ffn_hidden, 2 * b + 2)
                    nc.scalar.activation(xT[:, :], p_xT[:, 0:KE * P], ACT.Copy).then_inc(xT_made, 1)
                if inside(b):
                    e = act.value_load(expert_of[0:1, ds(b, 1)], min_val=0, max_val=EXPERTS - 1)
                    if later(b):
                        act.wait_ge(ffn_done, b)
                    for f in range(KH):
                        if f % 4 == 0:
                            act.wait_ge(h_turned, 2 * b + 1 + f // 4)
                        ins = nc.scalar.activation(hT[:, f * P:(f + 1) * P],
                                                   p_hT[f // 4][:, f % 4 * P:(f % 4 + 1) * P],
                                                   ACT.Gelu_apprx_tanh, bias=b1_sb[:, ds(e * KH + f, 1)])
                    ins.then_inc(gelu_made, 1)

            block_steps(act, block_step)

        @block.tensor
        def _(pe):
            mm, turn = nc.tensor.matmul, nc.tensor.transpose

            def embed(g):
                pe.wait_ge(patches_loaded, 16 * g + 16)
                if later(g, 2):
                    pe.wait_ge(v_copied, g - 1)
                if later(g):
                    pe.wait_ge(hidden_made, g)
                for k in range(KP):
                    ins = mm(p_h, patch_sb[:, k * T:(k + 1) * T], w_embed_sb[:, k * EMBED:(k + 1) * EMBED],
                             start=(k == 0), stop=(k == KP - 1))
                ins.then_inc(embedded, 1)

            def turn_normed(g):
                pe.wait_ge(normed_made, g + 1)
                if later(g):
                    pe.wait_ge(normedT_made, g)
                if later(g, 5):
                    pe.wait_ge(own_rank, 4 * (g - 4))
                for c in range(KE):
                    ins = turn(p_nT[:, c * T:(c + 1) * T], normed[0:T, c * P:(c + 1) * P], ident[0:T, 0:T])
                ins.then_inc(normed_turned, 1)

            def project_qk(g):
                pe.wait_ge(normedT_made, g + 1)
                if later(g):
                    pe.wait_ge(k_copied, g)
                for m in range(4):
                    for k in range(KE):
                        ins = mm((p_q if m < 2 else p_k)[:, m % 2 * T:(m % 2 + 1) * T],
                                 w_qk_sb[:, (k * 4 + m) * P:(k * 4 + m + 1) * P],
                                 normedT[:, k * T:(k + 1) * T], start=(k == 0), stop=(k == KE - 1))
                ins.then_inc(k_made, 1)

            def project_v(g):
                pe.wait_ge(hidden_made, up_to(g + 2))
                if later(g):
                    pe.wait_ge(v_copied, g)
                for k in range(KE):
                    ins = mm(p_v, normedT[:, k * T:(k + 1) * T], w_v_sb[:, k * EMBED:(k + 1) * EMBED],
                             start=(k == 0), stop=(k == KE - 1))
                ins.then_inc(v_made, 1)

            def score(g, half):
                if half == 0:
                    pe.wait_ge(k_copied, g + 1)
                for r in (2 * half, 2 * half + 1):
                    if later(g):
                        pe.wait_ge(probsT_made, 4 * g - 3 + r)
                    mm(scores[r][0:T, 0:4 * T], ident_b, causal, start=True, stop=False, skip_group_check=True)
                for j in range(4):
                    c, parity = j // 2, j % 2
                    for r in (2 * half, 2 * half + 1):
                        ins = mm(scores[r][0:T, j * T:(j + 1) * T],
                                 qT[32 * r:32 * r + 32, c * T:(c + 1) * T],
                                 kT[parity][32 * r:32 * r + 32, c * T:(c + 1) * T],
                                 start=False, stop=True, skip_group_check=True)
                ins.then_inc(scored, 1)

            def turn_probs(g):
                for r in range(4):
                    pe.wait_ge(probs_made, 4 * g + r + 1)
                    for j in range(4):
                        n = 4 * r + j
                        ins = turn(scores[r][0:T, j * T:(j + 1) * T], probs[0:T, n * T:(n + 1) * T],
                                   ident[0:T, 0:T])
                    ins.then_inc(probs_turned, 1)

            def turn_inverse(g):
                pe.wait_ge(inverse_made, g + 1)
                for c in range(KE):
                    ins = turn(p_inverseT[:, c * T:(c + 1) * T], inverse_wide[0:T, c * P:(c + 1) * P], ident[0:T, 0:T])
                ins.then_inc(inverse_turned, 1)

            def weigh(g, place):
                pe.wait_ge(v_copied, g + 1)
                if later(g):
                    pe.wait_ge(attn_made, g)
                for n in range(HEADS):
                    if n % 4 == 0:
                        pe.wait_ge(probsT_made, 4 * g + n // 4 + 1)
                    h, r, c = head_of(n), n // 4, n % 4 // 2
                    first = 2 * HEAD * h - HEAD * (n % 2)
                    ins = mm(p_oT[32 * r:32 * r + 32, c * T:(c + 1) * T], values[place][0:T, first:first + 2 * HEAD],
                             probsT[0:T, n * T:(n + 1) * T], start=(n % 2 == 0), stop=(n % 2 == 1))
                ins.then_inc(weighed, 1)

            def project_out(g):
                pe.wait_ge(weightedT_made, g + 1)
                for k in range(KE):
                    ins = mm(p_y, weightedT[:, k * T:(k + 1) * T], w_o_sb[:, k * EMBED:(k + 1) * EMBED],
                             start=(k == 0), stop=(k == KE - 1))
                ins.then_inc(projected, 1)

            def turn_normed2(g):
                pe.wait_ge(normed2_made, g + 1)
                if later(g):
                    pe.wait_ge(own_rank, 4 * g)
                for c in range(KE):
                    ins = turn(p_n2T[:, c * T:(c + 1) * T], payload[0:T, EMBED + c * P:EMBED + (c + 1) * P],
                               ident[0:T, 0:T])
                ins.then_inc(normed2_turned, 1)

            def route(g):
                pe.wait_ge(normed2T_made, g + 1)
                for k in range(KE):
                    ins = mm(p_logits, normed2T[:, k * T:(k + 1) * T], w_switch_sb[:, k * EXPERTS:(k + 1) * EXPERTS],
                             start=(k == 0), stop=(k == KE - 1))
                ins.then_inc(logits_made, 1)

            def count(g):
                pe.wait_ge(route_steps, ROUTE_STEPS * g + 6)
                mm(p_rank, earlier, onehot[0:T, :], start=True, stop=True)
                mm(p_count, ones_b, onehot[0:T, :], start=True, stop=True).then_inc(ranked, 1)

            def step(t, place):
                if runs(t, 0):
                    embed(t)
                if isinstance(t, int) and t == 1:
                    pe.wait_ge(attn_loaded, 16 * ATTN_LOADS)
                    pe.wait_ge(dve_ready, 7)
                if runs(t, 2):
                    turn_probs(t - 2)
                if runs(t, 1):
                    project_qk(t - 1)
                if runs(t, 2):
                    weigh(t - 2, 1 - place)
                if runs(t, 1):
                    project_v(t - 1)
                if runs(t, 2):
                    turn_inverse(t - 2)
                if runs(t, 0):
                    turn_normed(t)
                if runs(t, 4):
                    turn_normed2(t - 4)
                if runs(t, 1):
                    score(t - 1, 0)
                if runs(t, 4):
                    route(t - 4)
                if runs(t, 1):
                    score(t - 1, 1)
                if runs(t, 2):
                    project_out(t - 2)
                if runs(t, 4):
                    count(t - 4)

            pe.wait_ge(w_embed_loaded, 16)
            pe.wait_ge(embed_loaded, 16 * EMBED_LOADS)
            steps(pe, step)

            pe.wait_ge(ffn_loaded, 16 * (WEIGHT_LOADS + 1))
            pe.wait_ge(tables_steps, TABLE_STEPS)

            def block_step(b, r):
                if inside(b + 1):
                    pe.wait_ge(gathered[(r + 1) % RING], turns(b + 1))
                    if later(b, 0):
                        pe.wait_ge(xT_made, b + 1)
                    rows = gathered_rows[(r + 1) % RING]
                    for c in range(KE):
                        ins = turn(p_xT[:, c * P:(c + 1) * P], rows[:, EMBED + c * P:EMBED + (c + 1) * P],
                                   ident[:, :])
                    ins.then_inc(x_turned, 1)
                if inside(b - 1):
                    e = pe.value_load(expert_of[0:1, ds(b - 1, 1)], min_val=0, max_val=EXPERTS - 1)
                    pe.wait_ge(gelu_made, b)
                    if later(b - 1):
                        pe.wait_ge(ffn_read, b - 1)
                    for f in range(KH):
                        ins = mm(p_ffn[:, 0:EMBED], hT[:, f * P:(f + 1) * P],
                                 W[:, ds(W2_AT + e * KH * EMBED + f * EMBED, EMBED)],
                                 start=(f == 0), stop=(f == KH - 1))
                    ins.then_inc(ffn_done, 1)
                if inside(b):
                    for f in range(KH):
                        if f % 4 == 0:
                            pe.wait_ge(h1_copied, 2 * b + 1 + f // 4)
                        ins = turn(p_hT[f // 4][:, f % 4 * P:(f % 4 + 1) * P], h1[:, f * P:(f + 1) * P], ident[:, :])
                        if f % 4 == 3:
                            ins.then_inc(h_turned, 1)
                if inside(b + 1):
                    e = pe.value_load(expert_of[0:1, ds(b + 1, 1)], min_val=0, max_val=EXPERTS - 1)
                    pe.wait_ge(xT_made, b + 2)
                    for half in range(2):
                        for k in range(KE):
                            ins = mm(p_h1[half][:, :], xT[:, k * P:(k + 1) * P],
                                     W[:, ds(e * KE * HIDDEN + k * HIDDEN + half * 512, 512)],
                                     start=(k == 0), stop=(k == KE - 1))
                        ins.then_inc(ffn_hidden, 1)

            block_steps(pe, block_step)

        @block.vector
        def _(dve):
            v = nc.vector

            def settled():
                dve.sem_inc(dve_passed)

            def mean(i):
                return moments[0:T, 2 * i:2 * i + 1]

            def layer_stats(i, rows, made, g, stats_sem, moments_sem):
                dve.wait_ge(made, g + 1)
                settled()
                v.bn_stats(stats[0:T, 6 * i:6 * i + 6], rows).then_inc(stats_sem, 1)
                dve.wait_ge(stats_sem, g + 1)
                settled()
                v.bn_aggr(moments[0:T, 2 * i:2 * i + 2], stats[0:T, 6 * i:6 * i + 6]).then_inc(moments_sem, 1)

            def embed_rows(g):
                dve.wait_ge(embedded, g + 1)
                v.tensor_tensor(hidden_of(g), p_h, position_sb[0:T, :], ALU.add) \
                    .then_inc(hidden_made, 1)
                layer_stats(0, hidden_of(g), hidden_made, g, a_stats, a_moments)

            def inverse_deviations(t):
                for stage, moments_sem in ((0, a_moments), (3, c_moments), (4, d_moments)):
                    if runs(t, stage):
                        dve.wait_ge(moments_sem, t - stage + 1)
                n = [RSTD_STEPS * t]

                def link(ins):
                    n[0] = n[0] + 1
                    ins.then_inc(rstd_steps, 1)
                    dve.wait_ge(rstd_steps, n[0])

                square, factor = newton[0:T, 0:3], newton[0:T, 3:6]
                x, y = var_eps[0:T, :], rstd[0:T, :]
                variance = moments[0:T, :].rearrange("p (i c) -> p i c", c=2)[:, :, 1]
                link(v.tensor_scalar(x, variance, EPS, None, ALU.add))
                link(v.tensor_scalar(square.bitcast(i32), x.bitcast(i32), 1, None, ALU.logical_shift_right))
                link(v.tensor_scalar(y.bitcast(i32), square.bitcast(i32), -1.0, float(0x5F3759DF),
                                     ALU.mult, ALU.add))
                for _ in range(3):
                    link(v.tensor_tensor(square, y, y, ALU.mult))
                    link(v.scalar_tensor_tensor(square, square, -0.5, x, ALU.mult, ALU.mult))
                    link(v.scalar_tensor_tensor(y, square, 1.5, y, ALU.add, ALU.mult))

            def normalize(g):
                if later(g):
                    dve.wait_ge(normed_turned, g)
                v.tensor_scalar(normed[0:T, :], hidden_of(g), mean(0), rstd[0:T, 0:1],
                                ALU.subtract, ALU.mult).then_inc(normed_made, 1)

            def normalize2(g):
                if later(g):
                    dve.wait_ge(rows_written, 16 * g)
                    dve.wait_ge(normed2_turned, g)
                v.tensor_scalar(payload[0:T, EMBED:2 * EMBED], hidden_of(g), mean(2),
                                rstd[0:T, 2:3], ALU.subtract, ALU.mult).then_inc(normed2_made, 1)

            def add_residual(g):
                dve.wait_ge(beta_added, g + 1)
                dve.wait_ge(attn_g_made, g + 1)
                h = hidden_of(g)
                v.scalar_tensor_tensor(h, attn_g[0:T, :], rstd[0:T, 1:2], h, ALU.mult, ALU.add) \
                    .then_inc(residual_made, 1)
                layer_stats(2, h, residual_made, g, d_stats, d_moments)

            def find_top(g, half):
                if half == 0 and later(g):
                    dve.wait_ge(probs_made, 4 * g)
                dve.wait_ge(scored, 2 * g + half + 1)
                for r in (2 * half, 2 * half + 1):
                    v.tensor_reduce(best_score[0:T, 4 * r:4 * r + 4],
                                    scores[r][0:T, 0:4 * T].rearrange("p (j s) -> p j s", s=T),
                                    AX.X, ALU.max).then_inc(top_read, 1)
                dve.wait_ge(top_read, 4 * g + 2 * half + 2)
                v.tensor_scalar(top[0:T, 8 * half:8 * half + 8], best_score[0:T, 8 * half:8 * half + 8],
                                -SCALE, None, ALU.mult).then_inc(top_found, 1)

            def copy_values(g, place):
                dve.wait_ge(v_made, g + 1)
                v.tensor_tensor(values[place][0:T, :].rearrange("p (h d) -> p h d", h=HEADS)[:, :, 0:HEAD],
                                p_v.rearrange("p (h d) -> p h d", h=HEADS),
                                bv.rearrange("p (h d) -> p h d", h=HEADS), ALU.add).then_inc(v_copied, 1)

            def invert(g):
                dve.wait_ge(probs_made, 4 * g + 4)
                if later(g):
                    dve.wait_ge(inverse_made, g)
                v.reciprocal(inverse[0:T, :], sums[0:T, :]).then_inc(inverted, 1)

            def widen_inverse(g):
                dve.wait_ge(inverted, g + 1)
                if later(g):
                    dve.wait_ge(inverse_turned, g)
                v.tensor_copy(inverse_wide[0:T, :].rearrange("p (h d) -> p h d", h=HEADS),
                              inverse[0:T, :].unsqueeze(2).broadcast_to([T, HEADS, HEAD])).then_inc(inverse_made, 1)

            def divide(g):
                dve.wait_ge(inverseT_made, g + 1)
                if later(g):
                    dve.wait_ge(projected, g)
                v.tensor_tensor(weightedT[:, :], p_oT, inverseT[:, :], ALU.mult).then_inc(weightedT_made, 1)

            def attention_rows(g):
                dve.wait_ge(projected, g + 1)
                v.tensor_tensor(attn[0:T, :], p_y, bo, ALU.add).then_inc(attn_made, 1)
                layer_stats(1, attn[0:T, :], attn_made, g, c_stats, c_moments)
                dve.wait_ge(c_moments, g + 1)
                v.scalar_tensor_tensor(attn_g[0:T, :], attn[0:T, :], mean(1), gamma, ALU.subtract, ALU.mult) \
                    .then_inc(attn_g_made, 1)

            def pick(g):
                n = ROUTE_STEPS * g
                z = shifted[0:T, :]
                dve.wait_ge(logits_made, g + 1)
                v.tensor_tensor(logits[0:T, :], p_logits, b_switch_sb[0:T, :], ALU.add).then_inc(route_steps, 1)
                dve.wait_ge(route_steps, n + 1)
                v.tensor_reduce(best[0:T, 0:1], logits[0:T, :], AX.X, ALU.max).then_inc(route_steps, 1)
                dve.wait_ge(route_steps, n + 2)
                if later(g):
                    dve.wait_ge(numer_made, g)
                v.tensor_scalar(z, logits[0:T, :], best[0:T, 0:1], None, ALU.subtract).then_inc(route_steps, 1)
                dve.wait_ge(route_steps, n + 3)
                v.scalar_tensor_tensor(picks[0:T, :], z, 0.0, col("descending", T), ALU.is_equal, ALU.mult) \
                    .then_inc(route_steps, 1)
                dve.wait_ge(route_steps, n + 4)
                v.tensor_reduce(best[0:T, 1:2], picks[0:T, :], AX.X, ALU.max).then_inc(route_steps, 1)
                dve.wait_ge(route_steps, n + 5)
                if later(g):
                    dve.wait_ge(ranked, g)
                v.tensor_scalar(onehot[0:T, :], picks[0:T, :], best[0:T, 1:2], col("valid", T, g),
                                ALU.is_equal, ALU.mult).then_inc(route_steps, 1)

            def place_rows(g):
                dve.wait_ge(numer_made, g + 1)
                v.reciprocal(payload[0:T, 2 * EMBED:2 * EMBED + 1], best[0:T, 2:3]).then_inc(prob_made, 1)
                dve.wait_ge(ranked, g + 1)
                if later(g):
                    dve.wait_ge(own_rank, 4 * g)
                v.tensor_tensor(rank[0:T, :], p_rank, next_slot[0:T, :], ALU.add).then_inc(own_rank, 1)
                dve.wait_ge(own_rank, 4 * g + 1)
                v.tensor_tensor(rank_own[0:T, :], rank[0:T, :], onehot[0:T, :], ALU.mult).then_inc(own_rank, 1)
                dve.wait_ge(own_rank, 4 * g + 2)
                v.tensor_reduce(slot_f[0:T, :], rank_own[0:T, :], AX.X, ALU.add).then_inc(own_rank, 1)
                v.tensor_tensor(next_slot[:, :], p_count, next_slot[:, :], ALU.add).then_inc(own_rank, 1)
                dve.wait_ge(own_rank, 4 * g + 3)
                if later(g):
                    dve.wait_ge(ids_scattered, 16 * g)
                v.tensor_tensor(slot[0:T, :], slot_f[0:T, :], col("trash_slot", T, g), ALU.add) \
                    .then_inc(route_steps, 1)

            def step(t, place):
                if runs(t, 2):
                    invert(t - 2)
                if runs(t, 0):
                    embed_rows(t)
                if isinstance(t, int) and t == 1:
                    dve.wait_ge(attn_loaded, 16 * ATTN_LOADS)
                    v.tensor_copy(masks_sb[0:T, :], big[0:T, 0:masks_sb.shape[1]]).then_inc(dve_ready, 1)
                    for parity, name in enumerate(("even", "odd")):
                        v.tensor_scalar(k_bias[:, KE * parity:KE * (parity + 1)], b_qk_sb[:, KE:2 * KE],
                                        col(name), None, ALU.mult).then_inc(dve_ready, 1)
                inverse_deviations(t)
                if runs(t, 0):
                    normalize(t)
                if runs(t, 2):
                    widen_inverse(t - 2)
                if runs(t, 4):
                    normalize2(t - 4)
                if runs(t, 1):
                    copy_values(t - 1, place)
                if runs(t, 2):
                    divide(t - 2)
                if runs(t, 3):
                    add_residual(t - 3)
                if runs(t, 1):
                    find_top(t - 1, 0)
                if runs(t, 4):
                    pick(t - 4)
                if runs(t, 1):
                    find_top(t - 1, 1)
                if runs(t, 4):
                    place_rows(t - 4)
                if runs(t, 2):
                    attention_rows(t - 2)

            v.memset(moments[:, :], 1.0).then_inc(dve_ready, 1)
            v.memset(values[0][:, :], 0.0)
            v.memset(values[1][:, :], 0.0).then_inc(dve_ready, 1)
            dve.wait_ge(dve_ready, 2)
            dve.wait_ge(embed_loaded, 16 * EMBED_LOADS)
            v.tensor_copy(next_slot[:, :], col("first_slot")).then_inc(dve_ready, 1)
            v.tensor_tensor(position_sb[0:T, :], position_sb[0:T, :], first_row_sb[0:T, :], ALU.add) \
                .then_inc(dve_ready, 1)
            dve.wait_ge(dve_ready, 4)
            steps(dve, step)

            n = [0]

            def link(ins):
                n[0] += 1
                ins.then_inc(tables_steps, 1)
                dve.wait_ge(tables_steps, n[0])

            def cube(ap, mid, last):
                return ap.rearrange("p (a b) -> p a b", b=last)

            def over(ap, mid, last):
                return ap.unsqueeze(2).broadcast_to([P, mid, last])

            def each_row(ap, mid, last):
                return ap.unsqueeze(1).broadcast_to([P, mid, last])

            E, B = EXPERTS, BLOCKS
            counts, needs, ends, starts = (t8[:, i * E:(i + 1) * E] for i in range(4))
            number, own, start_of, count_of, last_of, at = (t17[:, i * B:(i + 1) * B] for i in range(6))
            wide = scratch[:, 0:E * THRESH]
            dve.wait_ge(own_rank, 4 * GROUPS)
            link(v.tensor_tensor(counts, next_slot[:, :], col("first_slot"), ALU.subtract))
            link(v.tensor_tensor(cube(wide, E, THRESH), over(counts, E, THRESH),
                                 cube(col("threshold"), E, THRESH), ALU.is_gt))
            link(v.tensor_reduce(needs, cube(wide, E, THRESH), AX.X, ALU.add))
            square = scratch[:, 0:E * E]
            link(v.tensor_tensor(cube(square, E, E), each_row(needs, E, E), cube(col("upto"), E, E), ALU.mult))
            link(v.tensor_reduce(ends, cube(square, E, E), AX.X, ALU.add))
            link(v.tensor_tensor(starts, ends, needs, ALU.subtract))
            link(v.tensor_scalar(best[:, 3:4], ends[:, E - 1:E], -1.0, None, ALU.add))
            link(v.tensor_scalar(number, col("block"), best[:, 3:4], None, ALU.min))
            link(v.tensor_tensor(cube(scratch[:, :], B, E), each_row(ends, B, E), over(number, B, E), ALU.is_le))
            link(v.tensor_reduce(own, cube(scratch[:, :], B, E), AX.X, ALU.add))
            link(v.tensor_copy(expert_of[:, :], own))
            link(v.tensor_tensor(cube(of_block[:, :], B, E), over(own, B, E), each_row(col("expert"), B, E),
                                 ALU.is_equal))
            link(v.tensor_tensor(cube(scratch[:, :], B, E), cube(of_block[:, :], B, E), each_row(starts, B, E),
                                 ALU.mult))
            link(v.tensor_reduce(start_of, cube(scratch[:, :], B, E), AX.X, ALU.add))
            link(v.tensor_tensor(cube(scratch[:, :], B, E), cube(of_block[:, :], B, E), each_row(counts, B, E),
                                 ALU.mult))
            link(v.tensor_reduce(count_of, cube(scratch[:, :], B, E), AX.X, ALU.add))
            link(v.tensor_tensor(at, number, start_of, ALU.subtract))
            link(v.tensor_scalar(at, at, float(P), col("row"), ALU.mult, ALU.add))
            link(v.tensor_scalar(last_of, count_of, -1.0, None, ALU.add))
            link(v.tensor_tensor(last_of, at, last_of, ALU.min))
            link(v.scalar_tensor_tensor(source_rows[:, :], own, float(REGION), last_of, ALU.mult, ALU.add))
            link(v.tensor_tensor(at, at, count_of, ALU.is_lt))
            link(v.scalar_tensor_tensor(live[:, :], col("block"), ends[:, E - 1:E], at, ALU.is_lt, ALU.mult))
            assert n[0] == TABLE_STEPS

            def block_step(b, r):
                if inside(b):
                    if later(b):
                        dve.wait_ge(h_turned, 2 * b)
                    for half in range(2):
                        dve.wait_ge(ffn_hidden, 2 * b + half + 1)
                        v.tensor_copy(h1[:, half * 512:(half + 1) * 512], p_h1[half][:, :]).then_inc(h1_copied, 1)
                if inside(b - 1):
                    q = (r - 1) % RING
                    rows = gathered_rows[q]
                    e = dve.value_load(expert_of[0:1, ds(b - 1, 1)], min_val=0, max_val=EXPERTS - 1)
                    dve.wait_ge(ffn_done, b)
                    if later(b - 1):
                        dve.wait_ge(result_made, b - 1)
                        dve.wait_ge(target_made, b - 1)
                    v.tensor_tensor(ffn_sum[:, :], p_ffn[:, 0:EMBED], b2_sb[:, ds(e * EMBED, EMBED)], ALU.add) \
                        .then_inc(ffn_read, 1)
                    if later(b - 1, RING):
                        dve.wait_ge(stored, 16 * (b - RING))
                    v.scalar_tensor_tensor(target_f[:, :], rows[:, PAY - 1:PAY], col("trash_out"),
                                           live[:, ds(b - 1, 1)], ALU.subtract, ALU.mult).then_inc(target_diff, 1)
                    dve.wait_ge(target_diff, b)
                    v.tensor_tensor(target[:, q:q + 1], target_f[:, :], col("trash_out"), ALU.add) \
                        .then_inc(target_made, 1)
                    dve.wait_ge(ffn_read, b)
                    v.scalar_tensor_tensor(result[q], ffn_sum[:, :], rows[:, PAY - 2:PAY - 1], rows[:, 0:EMBED],
                                           ALU.mult, ALU.add).then_inc(result_made, 1)

            block_steps(dve, block_step)


def _constants():
    tab = np.zeros((P, TABLE_N), np.float32)
    row = np.arange(P)

    def put(name, value):
        a, b = TABLE[name]
        tab[:, a:b] = value

    put("even", (row % 32 < 16)[:, None])
    put("odd", (row % 32 >= 16)[:, None])
    put("trash_out", (ROWS + row)[:, None])
    put("row", row[:, None])
    put("descending", EXPERTS - np.arange(EXPERTS))
    put("first_slot", REGION * np.arange(EXPERTS))
    token = T * np.arange(GROUPS)[None, :] + row[:, None]
    put("valid", token < ROWS)
    put("trash_slot", (token >= ROWS) * (EXPERTS * REGION + row[:, None]))
    put("token", token)
    put("block", np.arange(BLOCKS))
    put("threshold", np.tile(P * np.arange(THRESH), EXPERTS))
    e = np.arange(EXPERTS)
    put("upto", (e[None, :] <= e[:, None]).reshape(-1))
    put("expert", e)
    t = np.arange(T)
    seen = (t[:, None] // TOKENS == t[None, :] // TOKENS) & (t[None, :] <= t[:, None])
    masks = np.concatenate([np.tile(np.where(seen, 0.0, MASKED), (1, 4)), t[:, None] < t[None, :],
                            np.ones((T, P)), np.eye(T)], axis=1).astype(np.float32)
    return tab, np.eye(P, dtype=np.float32), masks


def kernel(**inputs):
    import concourse.bacc as _bacc
    from concourse.bass_utils import run_bass_kernel_spmd as _run

    x = {k: np.asarray(a) for k, a in inputs.items()}

    def rows_first(w, k):
        return w.reshape(k, P, -1).transpose(1, 0, 2).reshape(P, -1)

    def everywhere(v, parts=P):
        return np.broadcast_to(v.reshape(1, -1), (parts, v.size))

    img = x["x"].reshape(IMAGES, CHANNELS, GRID, PATCH, GRID, PATCH).transpose(1, 3, 5, 0, 2, 4)
    filled = np.zeros((PIXELS, GROUPS * PER, TOKENS), np.float32)
    filled[:, :IMAGES, 1:] = img.reshape(PIXELS, IMAGES, TOKENS - 1)
    patches = filled.reshape(KP, P, GROUPS, T).transpose(2, 1, 0, 3).reshape(GROUPS, P, KP * T)
    first = np.concatenate([x["L0_tok_cls_token"].reshape(1, EMBED),
                            everywhere(x["L0_tok_b"], TOKENS - 1)])
    w_qk = np.concatenate([x["L0_attn_Wq"], x["L0_attn_Wk"]], axis=1)
    b_qk = np.concatenate([x["L0_attn_bq"], x["L0_attn_bk"]]).reshape(4, P).T
    w1 = x["L0_ffn_w1"].reshape(EXPERTS, KE, P, HIDDEN).transpose(2, 0, 1, 3).reshape(P, -1)
    w2 = x["L0_ffn_w2"].reshape(EXPERTS, KH, P, EMBED).transpose(2, 0, 1, 3).reshape(P, -1)
    tab, eye, masks = _constants()
    arrays = {
        "patches": patches,
        "w_embed": rows_first(x["L0_tok_W"].T, KP),
        "position": np.tile(x["L0_tok_pos_embedding"].reshape(TOKENS, EMBED), (PER, 1)),
        "first_row": np.tile(first, (PER, 1)),
        "w_qk": rows_first(w_qk, KE), "b_qk": b_qk,
        "w_v": rows_first(x["L0_attn_Wv"], KE), "w_o": rows_first(x["L0_attn_Wo"], KE),
        "rows4": everywhere(np.concatenate([x["L0_attn_bv"], x["L0_attn_bo"], x["L0_attn_gamma"],
                                            x["L0_attn_beta"]])),
        "w_switch": rows_first(x["L0_ffn_switch_w"], KE), "b_switch": everywhere(x["L0_ffn_switch_b"]),
        "b1": x["L0_ffn_b1"].reshape(EXPERTS * KH, P).T, "b2": everywhere(x["L0_ffn_b2"]),
        "experts": np.concatenate([w1, w2], axis=1),
        "table": tab, "identity": eye, "masks": masks,
        "no_ids": np.zeros((EXPERTS * REGION + P, 1), np.int32),
    }
    nc = _bacc.Bacc("TRN2", target_bir_lowering=False, num_devices=1)
    arrays = {k: np.ascontiguousarray(a) for k, a in arrays.items()}
    args = [nc.dram_tensor(f"in_{k}_dram", a.shape, mybir.dt.from_np(a.dtype), kind="ExternalInput").ap()
            for k, a in arrays.items()]
    out = nc.dram_tensor("out_0_dram", (ROWS + P, EMBED), mybir.dt.float32, kind="ExternalOutput").ap()
    vit_layer(nc, *args, out)
    r = _run(nc, [{f"in_{k}_dram": a for k, a in arrays.items()}], core_ids=[0])
    return r.results[0]["out_0_dram"][:ROWS].reshape(IMAGES, TOKENS, EMBED)
```

```python
import numpy as np
import concourse.bass as bass
from concourse import mybir
from contextlib import ExitStack

IMAGES, EMBED, PATCH, SIDE, CHANNELS = 32, 256, 16, 96, 3
GRID = SIDE // PATCH
TOKENS = GRID * GRID + 1
PIXELS = CHANNELS * PATCH * PATCH
PER = 3
GROUPS = -(-IMAGES // PER)
T = PER * TOKENS
ROWS = IMAGES * TOKENS
HEADS, HEAD = 16, 16
EXPERTS, HIDDEN = 8, 1024
P = 128
KP, KE, KH = PIXELS // P, EMBED // P, HIDDEN // P
BLOCKS = (ROWS + (P - 1) * EXPERTS) // P
REGION = ROWS
PAY = 2 * EMBED + 2
RING = 4
IN_FLIGHT = 6
VALUES = 2 * HEADS * HEAD
EPS = 1e-5
MASKED = -1e30
THRESH = -(-ROWS // P)

TABLE = {}


def _columns():
    at = 0
    for name, n in (("even", 1), ("odd", 1), ("trash_out", 1), ("descending", EXPERTS),
                    ("first_slot", EXPERTS), ("valid", GROUPS), ("trash_slot", GROUPS), ("token", GROUPS),
                    ("block", BLOCKS), ("block_row", BLOCKS), ("region_row", EXPERTS),
                    ("threshold", EXPERTS * THRESH), ("upto", EXPERTS * EXPERTS), ("expert", EXPERTS)):
        TABLE[name] = (at, at + n)
        at += n
    return at


TABLE_N = _columns()


def vit_layer(nc, patches, w_embed, position, first_row, w_qk, b_qk, w_v, w_o, rows4, w_switch, b_switch,
              b1, b2, experts, table, identity, masks, no_ids, out):
    f32, bf16, i32 = mybir.dt.float32, mybir.dt.bfloat16, mybir.dt.int32
    ALU, ACT, AX = mybir.AluOpType, mybir.ActivationFunctionType, mybir.AxisListType
    SCALE = float(HEAD) ** -0.5
    ds = bass.ds

    ctx = ExitStack()
    with ctx:
        def sb(name, cols, dt=f32, parts=P):
            return ctx.enter_context(nc.sbuf_tensor(name, [parts, cols], dt))

        def sem(name):
            return ctx.enter_context(nc.semaphore(name))

        W = sb("expert_weights", EXPERTS * 2 * KE * HIDDEN)
        W2_AT = EXPERTS * KE * HIDDEN
        second_patches = W[:, W.shape[1] - KP * T:W.shape[1]]
        tab = sb("table_sb", TABLE_N)
        ident = sb("ident", P)
        b1_sb = sb("b1_sb", EXPERTS * KH)
        b2_sb = sb("b2_sb", EXPERTS * EMBED)
        expert_of = sb("expert_of", BLOCKS, i32)
        source_rows = sb("source_rows", BLOCKS, i32)
        live = sb("live", BLOCKS)

        front = sb("front", KP * EMBED + KP * T)
        w_embed_sb, patch_sb = front[:, 0:KP * EMBED], front[:, KP * EMBED:KP * (EMBED + T)]
        gathered_rows = [front[:, i * PAY:(i + 1) * PAY] for i in range(RING)]
        position_sb = sb("position_sb", EMBED)
        first_row_sb = sb("first_row_sb", EMBED)
        attention_weights = sb("attention_weights", KE * HIDDEN)
        w_qk_sb, w_v_sb, w_o_sb = (attention_weights[:, i * EMBED:j * EMBED]
                                   for i, j in ((0, 2 * KE), (2 * KE, 3 * KE), (3 * KE, 4 * KE)))
        b_qk_sb = sb("b_qk_sb", 4)
        k_bias = sb("k_bias", 2 * KE)
        q_bias = sb("q_bias", KE)
        rows4_sb = sb("rows4_sb", 4 * EMBED)
        bv, bo, gamma, beta = (rows4_sb[0:T, i * EMBED:(i + 1) * EMBED] for i in range(4))
        w_switch_sb = sb("w_switch_sb", KE * EXPERTS)
        b_switch_sb = sb("b_switch_sb", EXPERTS)
        masks_sb = sb("masks_sb", 4 * T + T + P + T, bf16)
        causal, earlier = masks_sb[0:T, 0:4 * T], masks_sb[0:T, 4 * T:5 * T]
        ones_b, ident_b = masks_sb[0:T, 5 * T:5 * T + P], masks_sb[0:T, 5 * T + P:6 * T + P]

        token_rows = sb("token_rows", KE * HIDDEN)
        hidden, attn, attn_g = (token_rows[:, i * EMBED:j * EMBED] for i, j in (
            (0, IN_FLIGHT), (IN_FLIGHT, IN_FLIGHT + 1), (IN_FLIGHT + 1, IN_FLIGHT + 2)))
        normed = sb("normed", EMBED)
        normedT = sb("normedT", KE * T)
        qT = sb("qT", KE * T)
        kT = sb("kT", 2 * KE * T)
        values = [sb(f"values_{i}", VALUES) for i in range(2)]
        big = sb("big", 2 * HEADS * T)
        probs, probsT = big[:, 0:HEADS * T], big[:, HEADS * T:2 * HEADS * T]
        sums = sb("sums", HEADS)
        inverse = sb("inverse", HEADS)
        inverse_wide = sb("inverse_wide", EMBED)
        inverseT = sb("inverseT", KE * T)
        weightedT = sb("weightedT", KE * T)
        payload = [sb(f"payload_{i}", PAY) for i in range(2)]
        normed2T = sb("normed2T", KE * T)
        stats = sb("stats", 18)
        moments = sb("moments", 6)
        var_eps = sb("var_eps", 3)
        rstd = sb("rstd", 3)
        newton = sb("newton", 6)
        top = sb("top", HEADS)
        best = sb("best", 4)
        negated = sb("negated", EXPERTS)
        numer = sb("numer", EXPERTS)
        picks = sb("picks", EXPERTS)
        onehot = sb("onehot", EXPERTS, bf16)
        rank = sb("rank", EXPERTS)
        rank_own = sb("rank_own", EXPERTS)
        next_slot = sb("next_slot", EXPERTS)
        slot_f = sb("slot_f", 1)
        slot = sb("slot", 2, i32)
        token_now = sb("token_now", 1, i32)

        xT = [sb(f"xT_{i}", KE * P) for i in range(2)]
        hT = [big[:, 0:HIDDEN], big[:, HIDDEN:2 * HIDDEN]]
        w1_now = [attention_weights, token_rows]
        result = [big[:, 2 * HIDDEN + i * EMBED:2 * HIDDEN + (i + 1) * EMBED] for i in range(RING)]
        ffn_sum = sb("ffn_sum", EMBED)
        source_now = sb("source_now", RING, i32)
        token_of = sb("token_of", RING, i32)
        target_f = sb("target_f", 1)
        unused = sb("unused", 1)
        zeros = sb("zeros", P)
        target = sb("target", RING, i32)
        scratch = sb("scratch", 2 * BLOCKS * EXPERTS)
        of_block = sb("of_block", BLOCKS * EXPERTS)
        of_experts = sb("of_experts", 5 * EXPERTS)
        of_blocks = sb("of_blocks", 4 * BLOCKS)

        bank = [ctx.enter_context(nc.psum_tensor(f"bank{i}", [P, 512], f32)) for i in range(8)]
        scores = bank[0:4]
        p_h, p_v = bank[4][0:T, 0:EMBED], bank[4][0:T, EMBED:2 * EMBED]
        p_q, p_k = bank[5][:, 0:KE * T], bank[5][:, KE * T:2 * KE * T]
        p_nT = bank[6][:, 0:KE * T]
        route_banks = [(b[:, KE * T:2 * KE * T], b[0:T, 480:488], b[0:T, 488:496], b[:, 496:504])
                       for b in (bank[6], bank[0])]
        n2T_places = [normed2T, normedT]
        p_oT, p_inverseT = bank[7][:, 0:KE * T], bank[7][:, EMBED:EMBED + KE * T]
        p_y = bank[7][0:T, EMBED:2 * EMBED]
        p_hT, p_ffn, p_xT = (bank[0:2], bank[2:4]), (bank[4], bank[6]), bank[5]

        def col(name, parts=P, at=None):
            a, b = TABLE[name]
            if at is None:
                return tab[0:parts, a:b]
            return tab[0:parts, ds(a + at, 1)]

        EMBED_PIECES = 3
        w_embed_loaded = [sem(f"w_embed_loaded_{i}") for i in range(EMBED_PIECES)]
        embed_loaded, qk_loaded, attn_loaded, ffn_loaded = (
            sem("embed_loaded"), sem("qk_loaded"), sem("attn_loaded"), sem("ffn_loaded"))
        second_patches_loaded = sem("second_patches_loaded")
        patches_loaded, embedded, hidden_made = sem("patches_loaded"), sem("embedded"), sem("hidden_made")
        dve_ready = sem("dve_ready")
        a_stats, a_moments = sem("a_stats"), sem("a_moments")
        rstd_steps, normed_made = sem("rstd_steps"), sem("normed_made")
        normed_turned, normedT_made = sem("normed_turned"), sem("normedT_made")
        k_made, v_made, k_copied, v_copied = sem("k_made"), sem("v_made"), sem("k_copied"), sem("v_copied")
        scored, top_found, probs_made = sem("scored"), sem("top_found"), sem("probs_made")
        probs_turned, probsT_made = sem("probs_turned"), sem("probsT_made")
        inverted, inverse_made, inverse_turned, inverseT_made, weighed, weightedT_made = (
            sem("inverted"), sem("inverse_made"), sem("inverse_turned"), sem("inverseT_made"),
            sem("weighed"), sem("weightedT_made"))
        projected, attn_made, c_stats, c_moments, attn_g_made = (
            sem("projected"), sem("attn_made"), sem("c_stats"), sem("c_moments"), sem("attn_g_made"))
        beta_added, residual_made, d_stats, d_moments = (
            sem("beta_added"), sem("residual_made"), sem("d_stats"), sem("d_moments"))
        normed2_made, normed2_turned, normed2T_made = (
            sem("normed2_made"), sem("normed2_turned"), sem("normed2T_made"))
        logits_made, route_steps, numer_made = sem("logits_made"), sem("route_steps"), sem("numer_made")
        ranked, payload_copied = sem("ranked"), sem("payload_copied")
        ids_cleared, token_set, ids_scattered, rows_written = (
            sem("ids_cleared"), sem("token_set"), sem("ids_scattered"), sem("rows_written"))
        tables_steps = sem("tables_steps")
        source_set = sem("source_set")
        ids_gathered, gathered = (
            [sem(f"{name}_{r}") for r in range(RING)] for name in ("ids_gathered", "gathered"))
        stored = sem("stored")
        x_turned, xT_made, w1_copied, ffn_hidden, gelu_made = (
            sem("x_turned"), sem("xT_made"), sem("w1_copied"), sem("ffn_hidden"), sem("gelu_made"))
        ffn_done, ffn_read, target_diff, target_made, result_made = (
            sem("ffn_done"), sem("ffn_read"), sem("target_diff"), sem("target_made"), sem("result_made"))
        prob_made = sem("prob_made")
        sp_passed, pool_passed, dve_passed = sem("sp_passed"), sem("pool_passed"), sem("dve_passed")
        own_rank = sem("own_rank")
        rows_dram = nc.dram_tensor("rows_dram", (GROUPS * T, PAY), f32).ap()
        ids_dram = nc.dram_tensor("ids_dram", (EXPERTS * REGION + P, 1), i32).ap()

        EMBED_LOADS, QK_LOADS, ATTN_LOADS = 3, 4, 6
        WEIGHT_LOADS = 16
        RSTD_STEPS, ROUTE_STEPS = 12, 6
        TABLE_STEPS = 16
        SOURCE_STEPS = 15
        START_PRODUCTS, WAIT_PRODUCTS, FETCH_PRODUCTS = 8, 6, 17
        LAST = GROUPS + 4
        FULL = 5
        STEADY = RING + 1
        TURNS = (BLOCKS - 2 - STEADY) // RING

        def hidden_of(g):
            return hidden[0:T, ds(g % IN_FLIGHT * EMBED, EMBED)]

        def head_of(n):
            r, j = n // 4, n % 4
            return j // 2 * (P // HEAD) + 2 * r + j % 2

        def runs(t, stage):
            return not isinstance(t, int) or 0 <= t - stage < GROUPS

        def later(g, n=1):
            return not isinstance(g, int) or g >= n

        def steps(eng, step, finish):
            for t in range(FULL):
                step(t, t % 2)
            with eng.Fori(0, (GROUPS - FULL) // 2) as turn:
                for i in range(2):
                    step(turn * 2 + FULL + i, (FULL + i) % 2)
            step(GROUPS, GROUPS % 2)
            finish()

        def block_steps(eng, step):
            for b in range(-1, STEADY):
                step(b, b % RING)
            with eng.Fori(0, TURNS) as turn:
                for i in range(RING):
                    step(turn * RING + STEADY + i, (STEADY + i) % RING)
            for b in range(STEADY + TURNS * RING, BLOCKS + 1):
                step(b, b % RING)

        G = GROUPS - 1
        assert (GROUPS - FULL) % 2 == 0 and G % 2 == 0

        def up_to(count):
            return min(count, GROUPS) if isinstance(count, int) else count

        def turns(b):
            return 16 * (b // RING) + 16

        def inside(b):
            return not isinstance(b, int) or 0 <= b < BLOCKS

        block = ctx.enter_context(nc.Block())

        @block.sync
        def _(sp):
            sp.dma_start(patch_sb, patches[0, :, :]).then_inc(patches_loaded, 16)
            for i in range(EMBED_PIECES):
                piece = slice(i * KP * EMBED // EMBED_PIECES, (i + 1) * KP * EMBED // EMBED_PIECES)
                sp.dma_start(w_embed_sb[:, piece], w_embed[:, piece]).then_inc(w_embed_loaded[i], 16)
            sp.dma_start(position_sb[0:T, :], position).then_inc(embed_loaded, 16)
            sp.dma_start(first_row_sb[0:T, :], first_row).then_inc(embed_loaded, 16)
            sp.dma_start(ident[:, :], identity).then_inc(embed_loaded, 16)
            sp.dma_start(second_patches, patches[1, :, :]).then_inc(second_patches_loaded, 16)
            for dst, src in ((w_qk_sb, w_qk), (b_qk_sb, b_qk), (tab, table)):
                sp.dma_start(dst[:, :], src).then_inc(qk_loaded, 16)
            sp.dma_start(big[0:T, 0:masks_sb.shape[1]], masks).then_inc(qk_loaded, 16)
            for dst, src in ((w_v_sb, w_v), (rows4_sb, rows4), (w_o_sb, w_o), (w_switch_sb, w_switch),
                             (b_switch_sb, b_switch), (b1_sb, b1)):
                sp.dma_start(dst[:, :], src).then_inc(attn_loaded, 16)

            sp.dma_start(ids_dram, no_ids).then_inc(ids_cleared, 16)
            sp.dma_start(b2_sb[:, :], b2).then_inc(ffn_loaded, 16)

            def load_patches(g):
                sp.wait_ge(embedded, g)
                sp.dma_start(patch_sb, patches[ds(g, 1), :, :].rearrange("a p n -> (a p) n")) \
                    .then_inc(patches_loaded, 16)

            each = W.shape[1] // WEIGHT_LOADS
            early = WEIGHT_LOADS - (GROUPS - FULL)

            def load_weights(n):
                sp.dma_start(W[:, ds(n * each, each)], experts[:, ds(n * each, each)]).then_inc(ffn_loaded, 16)

            def write_rows(g, place):
                sp.wait_ge(payload_copied, 2 * g + 2)
                sp.sem_inc(sp_passed)
                sp.wait_ge(prob_made, g + 1)
                sp.sem_inc(sp_passed)
                sp.wait_ge(normed2_made, g + 1)
                if later(g):
                    sp.sem_inc(sp_passed)
                    sp.wait_ge(rows_written, 16 * g)
                sp.dma_start(rows_dram[ds(g * T, T), :], payload[place][0:T, :]).then_inc(rows_written, 16)

            def step(t, place):
                if runs(t + 1, 0) and not (isinstance(t, int) and t == 0):
                    load_patches(t + 1)
                if not isinstance(t, int):
                    load_weights(early + t - FULL)
                elif 1 <= t < FULL:
                    for n in range(early * (t - 1) // (FULL - 1), early * t // (FULL - 1)):
                        load_weights(n)
                if runs(t, 4):
                    write_rows(t - 4, place)

            for t in range(FULL):
                step(t, t % 2)
            with sp.Fori(0, (GROUPS - FULL) // 2 - 1) as turn:
                for i in range(2):
                    step(turn * 2 + FULL + i, (FULL + i) % 2)
            for n in range(WEIGHT_LOADS - 2, WEIGHT_LOADS):
                load_weights(n)
            for t in range(GROUPS - 2, LAST):
                step(t, t % 2)

        @block.gpsimd
        def _(pool):
            def settled():
                pool.sem_inc(pool_passed)

            def add_beta(g):
                pool.wait_ge(normed_made, g + 1)
                settled()
                h = hidden_of(g)
                nc.gpsimd.tensor_tensor(h, h, beta, ALU.add).then_inc(beta_added, 1)

            def fill_payload(g, place):
                if later(g, 2):
                    pool.wait_ge(rows_written, 16 * (g - 1))
                    settled()
                pool.wait_ge(d_stats, g + 1)
                settled()
                nc.gpsimd.tensor_copy(payload[place][0:T, 0:EMBED], hidden_of(g)).then_inc(payload_copied, 1)
                nc.gpsimd.tensor_copy(payload[place][0:T, PAY - 1:PAY], col("token", T, g)) \
                    .then_inc(payload_copied, 1)

            def scatter_ids(g, place):
                if later(g):
                    pool.wait_ge(ids_scattered, 16 * g)
                    settled()
                nc.gpsimd.tensor_copy(token_now[0:T, :], col("token", T, g)).then_inc(token_set, 1)
                pool.wait_ge(token_set, g + 1)
                settled()
                pool.wait_ge(route_steps, ROUTE_STEPS * g + ROUTE_STEPS)
                settled()
                slots = bass.IndirectOffsetOnAxis(slot[0:T, place:place + 1], 0)
                nc.gpsimd.indirect_dma_start(ids_dram[:, :], slots, token_now[0:T, :], None).then_inc(ids_scattered, 16)

            def step(t, place):
                if runs(t, 4):
                    fill_payload(t - 4, place)
                if runs(t, 1):
                    add_beta(t - 1)
                if runs(t, 4):
                    scatter_ids(t - 4, place)

            def finish():
                fill_payload(G - 2, 0)
                fill_payload(G - 1, 1)
                scatter_ids(G - 2, 0)
                fill_payload(G, 0)
                scatter_ids(G - 1, 1)
                scatter_ids(G, 0)

            pool.wait_ge(qk_loaded, 16 * QK_LOADS)
            pool.wait_ge(attn_loaded, 16 * ATTN_LOADS)
            pool.wait_ge(ids_cleared, 16)
            steps(pool, step, finish)

            def find(b, r):
                if later(b, RING):
                    pool.wait_ge(gathered[r], turns(b - RING))
                    settled()
                if isinstance(b, int):
                    source = source_rows[:, b:b + 1]
                else:
                    source = source_now[:, r:r + 1]
                    nc.gpsimd.tensor_copy(source, source_rows[:, ds(b, 1)]).then_inc(source_set, 1)
                    pool.wait_ge(source_set, b - (STEADY + 2))
                    settled()
                nc.gpsimd.indirect_dma_start(token_of[:, r:r + 1], None, ids_dram[:, :],
                                             bass.IndirectOffsetOnAxis(source, 0)) \
                    .then_inc(ids_gathered[r], 16)

            def fetch(b, r):
                if later(b, RING):
                    pool.wait_ge(result_made, b - RING + 1)
                    settled()
                pool.wait_ge(ids_gathered[r], turns(b))
                settled()
                nc.gpsimd.indirect_dma_start(gathered_rows[r], None, rows_dram[:, :],
                                             bass.IndirectOffsetOnAxis(token_of[:, r:r + 1], 0)) \
                    .then_inc(gathered[r], 16)

            def store(b, r):
                if later(b):
                    pool.wait_ge(stored, 16 * b)
                    settled()
                pool.wait_ge(target_made, b + 1)
                settled()
                pool.wait_ge(result_made, b + 1)
                settled()
                nc.gpsimd.indirect_dma_start(out[:, :], bass.IndirectOffsetOnAxis(target[:, r:r + 1], 0),
                                             result[r], None).then_inc(stored, 16)

            pool.wait_ge(ids_scattered, 16 * GROUPS)
            pool.wait_ge(tables_steps, SOURCE_STEPS)
            find(0, 0)
            find(1, 1)
            pool.wait_ge(rows_written, 16 * GROUPS)
            fetch(0, 0)
            fetch(1, 1)
            find(2, 2)

            def block_step(b, r):
                if later(b, 0) and inside(b + 3):
                    find(b + 3, (r + 3) % RING)
                if later(b, 0) and inside(b + 2):
                    fetch(b + 2, (r + 2) % RING)
                if inside(b - 1):
                    store(b - 1, (r - 1) % RING)

            block_steps(pool, block_step)
            pool.wait_ge(stored, 16 * BLOCKS)

        @block.scalar
        def _(act):
            def copy_q_and_k(g):
                act.wait_ge(k_made, g + 1)
                if later(g):
                    act.wait_ge(scored, 2 * g)
                for c in range(KE):
                    at = slice(c * T, (c + 1) * T)
                    nc.scalar.activation(qT[:, at], p_q[:, at], ACT.Identity, bias=q_bias[:, c:c + 1],
                                         scale=SCALE)
                    for parity, name in enumerate(("even", "odd")):
                        to = (2 * c + parity) * T
                        ins = nc.scalar.activation(kT[:, to:to + T], p_k[:, at], ACT.Identity,
                                                   bias=k_bias[:, KE * parity + c:KE * parity + c + 1],
                                                   scale=col(name))
                ins.then_inc(k_copied, 1)

            def copy_probsT(g):
                if later(g):
                    act.wait_ge(weighed, g)
                for r in range(4):
                    act.wait_ge(probs_turned, 4 * g + r + 1)
                    nc.scalar.activation(probsT[0:T, r * 4 * T:(r + 1) * 4 * T], scores[r][0:T, 0:4 * T],
                                         ACT.Copy).then_inc(probsT_made, 1)

            def softmax(g, rs):
                if rs[0] == 0 and later(g):
                    act.wait_ge(probs_turned, 4 * g)
                    act.wait_ge(inverted, g)
                for r in rs:
                    act.wait_ge(top_found, 4 * g + 1 + r)
                    for j in range(4):
                        n = 4 * r + j
                        h = head_of(n)
                        ins = nc.scalar.activation(probs[0:T, n * T:(n + 1) * T], scores[r][0:T, j * T:(j + 1) * T],
                                                   ACT.Exp, bias=top[0:T, n:n + 1],
                                                   accum_out=sums[0:T, h:h + 1])
                    ins.then_inc(probs_made, 1)

            def copy_normedT(g):
                act.wait_ge(normed_turned, g + 1)
                if runs(g, 4):
                    act.wait_ge(normed2_turned, g - 3)
                if later(g):
                    act.wait_ge(v_made, g)
                nc.scalar.activation(normedT[:, :], p_nT, ACT.Copy).then_inc(normedT_made, 1)

            def copy_normed2T(g, other=0):
                act.wait_ge(normed2_turned, g + 1)
                if later(g):
                    act.wait_ge(logits_made, g)
                nc.scalar.activation(n2T_places[other][:, :], route_banks[other][0], ACT.Copy) \
                    .then_inc(normed2T_made, 1)

            def copy_inverseT(g):
                act.wait_ge(inverse_turned, g + 1)
                if later(g):
                    act.wait_ge(weightedT_made, g)
                nc.scalar.activation(inverseT[:, :], p_inverseT, ACT.Copy).then_inc(inverseT_made, 1)

            def route_numer(g):
                act.wait_ge(route_steps, ROUTE_STEPS * g + 2)
                if later(g):
                    act.wait_ge(route_steps, ROUTE_STEPS * g)
                nc.scalar.activation(numer[0:T, :], negated[0:T, :], ACT.Exp, bias=best[0:T, 0:1], scale=-1.0,
                                     accum_out=best[0:T, 2:3]).then_inc(numer_made, 1)

            def step(t, place):
                if isinstance(t, int) and t == 1:
                    act.wait_ge(qk_loaded, 16 * QK_LOADS)
                    act.wait_ge(dve_ready, 8)
                if runs(t, 2):
                    copy_probsT(t - 2)
                if runs(t, 1):
                    copy_q_and_k(t - 1)
                if runs(t, 2):
                    copy_inverseT(t - 2)
                if runs(t, 0):
                    copy_normedT(t)
                if runs(t, 4):
                    copy_normed2T(t - 4)
                if runs(t, 1):
                    softmax(t - 1, (0, 1))
                if runs(t, 4):
                    route_numer(t - 4)
                if runs(t, 1):
                    softmax(t - 1, (2, 3))

            def finish():
                copy_probsT(G)
                copy_inverseT(G)
                copy_normed2T(G - 2, 0)
                route_numer(G - 2)
                copy_normed2T(G - 1, 1)
                copy_normed2T(G, 0)
                route_numer(G - 1)
                route_numer(G)

            steps(act, step, finish)

            act.wait_ge(attn_loaded, 16 * ATTN_LOADS)
            nc.scalar.activation(unused[:, :], b1_sb[:, 0:1], ACT.Gelu_apprx_tanh)
            act.wait_ge(tables_steps, TABLE_STEPS)

            def block_step(b, r):
                e = None
                if inside(b):
                    e = act.value_load(expert_of[0:1, ds(b, 1)], min_val=0, max_val=EXPERTS - 1)
                for half in range(2):
                    if half == (1 if later(b) else 0) and inside(b + 1):
                        act.wait_ge(x_turned, b + 2)
                        if later(b):
                            act.wait_ge(ffn_hidden, 2 * b)
                        nc.scalar.activation(xT[(r + 1) % 2][:, :], p_xT[:, 0:KE * P], ACT.Copy) \
                            .then_inc(xT_made, 1)
                    if inside(b):
                        if later(b, 2):
                            act.wait_ge(ffn_done, b - 1)
                        act.wait_ge(ffn_hidden, 2 * b + 1 + half)
                        for j in range(4):
                            f = 4 * half + j
                            ins = nc.scalar.activation(hT[r % 2][:, f * P:(f + 1) * P],
                                                       p_hT[r % 2][half][:, j * P:(j + 1) * P],
                                                       ACT.Gelu_apprx_tanh, bias=b1_sb[:, ds(e * KH + f, 1)])
                        ins.then_inc(gelu_made, 1)

            block_steps(act, block_step)

        @block.tensor
        def _(pe):
            mm, turn = nc.tensor.matmul, nc.tensor.transpose

            def keep_clock(products):
                for _ in range(products):
                    mm(bank[6][:, 0:P], zeros[:, :], zeros[:, :], start=True, stop=True)

            def embed(g):
                second = isinstance(g, int) and g == 1
                if second:
                    pe.wait_ge(second_patches_loaded, 16)
                else:
                    pe.wait_ge(patches_loaded, 16 * g if later(g) else 16)
                pixels = second_patches if second else patch_sb
                if later(g, 2):
                    pe.wait_ge(v_copied, g - 1)
                if later(g):
                    pe.wait_ge(hidden_made, g)
                for k in range(KP):
                    if isinstance(g, int) and g == 0 and k % (KP // EMBED_PIECES) == 0:
                        pe.wait_ge(w_embed_loaded[k // (KP // EMBED_PIECES)], 16)
                    ins = mm(p_h, pixels[:, k * T:(k + 1) * T], w_embed_sb[:, k * EMBED:(k + 1) * EMBED],
                             start=(k == 0), stop=(k == KP - 1))
                ins.then_inc(embedded, 1)

            def turn_normed(g):
                pe.wait_ge(normed_made, g + 1)
                if later(g):
                    pe.wait_ge(normedT_made, g)
                if later(g, 5):
                    pe.wait_ge(own_rank, 4 * (g - 4))
                for c in range(KE):
                    ins = turn(p_nT[:, c * T:(c + 1) * T], normed[0:T, c * P:(c + 1) * P], ident[0:T, 0:T])
                ins.then_inc(normed_turned, 1)

            def project_qk(g):
                pe.wait_ge(normedT_made, g + 1)
                if later(g):
                    pe.wait_ge(k_copied, g)
                for m in range(4):
                    for k in range(KE):
                        ins = mm((p_q if m < 2 else p_k)[:, m % 2 * T:(m % 2 + 1) * T],
                                 w_qk_sb[:, (k * 4 + m) * P:(k * 4 + m + 1) * P],
                                 normedT[:, k * T:(k + 1) * T], start=(k == 0), stop=(k == KE - 1))
                ins.then_inc(k_made, 1)

            def project_v(g):
                pe.wait_ge(hidden_made, up_to(g + 2))
                if later(g):
                    pe.wait_ge(v_copied, g)
                for k in range(KE):
                    ins = mm(p_v, normedT[:, k * T:(k + 1) * T], w_v_sb[:, k * EMBED:(k + 1) * EMBED],
                             start=(k == 0), stop=(k == KE - 1))
                ins.then_inc(v_made, 1)

            def score(g, half):
                if half == 0:
                    pe.wait_ge(k_copied, g + 1)
                for r in (2 * half, 2 * half + 1):
                    if later(g):
                        pe.wait_ge(probsT_made, 4 * g - 3 + r)
                    mm(scores[r][0:T, 0:4 * T], ident_b, causal, start=True, stop=False, skip_group_check=True)
                for c in range(KE):
                    two = slice(2 * c * T, 2 * (c + 1) * T)
                    for r in (2 * half, 2 * half + 1):
                        ins = mm(scores[r][0:T, two], qT[32 * r:32 * r + 32, c * T:(c + 1) * T],
                                 kT[32 * r:32 * r + 32, two], start=False, stop=True, skip_group_check=True)
                ins.then_inc(scored, 1)

            def turn_probs(g):
                for r in range(4):
                    pe.wait_ge(probs_made, 4 * g + r + 1)
                    for j in range(4):
                        n = 4 * r + j
                        ins = turn(scores[r][0:T, j * T:(j + 1) * T], probs[0:T, n * T:(n + 1) * T],
                                   ident[0:T, 0:T])
                    ins.then_inc(probs_turned, 1)

            def turn_inverse(g):
                pe.wait_ge(inverse_made, g + 1)
                for c in range(KE):
                    ins = turn(p_inverseT[:, c * T:(c + 1) * T], inverse_wide[0:T, c * P:(c + 1) * P],
                               ident[0:T, 0:T])
                ins.then_inc(inverse_turned, 1)

            def weigh(g, place):
                pe.wait_ge(v_copied, g + 1)
                if later(g):
                    pe.wait_ge(attn_made, g)
                for n in range(HEADS):
                    if n % 4 == 0:
                        pe.wait_ge(probsT_made, 4 * g + n // 4 + 1)
                    h, r, c = head_of(n), n // 4, n % 4 // 2
                    first = 2 * HEAD * h - HEAD * (n % 2)
                    ins = mm(p_oT[32 * r:32 * r + 32, c * T:(c + 1) * T],
                             values[place][0:T, first:first + 2 * HEAD],
                             probsT[0:T, n * T:(n + 1) * T], start=(n % 2 == 0), stop=(n % 2 == 1))
                ins.then_inc(weighed, 1)

            def project_out(g):
                pe.wait_ge(weightedT_made, g + 1)
                for k in range(KE):
                    ins = mm(p_y, weightedT[:, k * T:(k + 1) * T], w_o_sb[:, k * EMBED:(k + 1) * EMBED],
                             start=(k == 0), stop=(k == KE - 1))
                ins.then_inc(projected, 1)

            def turn_normed2(g, place, counted, other=0):
                pe.wait_ge(normed2_made, g + 1)
                if later(counted):
                    pe.wait_ge(own_rank, 4 * counted)
                for c in range(KE):
                    ins = turn(route_banks[other][0][:, c * T:(c + 1) * T],
                               payload[place][0:T, EMBED + c * P:EMBED + (c + 1) * P],
                               ident[0:T, 0:T])
                ins.then_inc(normed2_turned, 1)

            def route(g, other=0):
                pe.wait_ge(normed2T_made, g + 1)
                for k in range(KE):
                    ins = mm(route_banks[other][1], n2T_places[other][:, k * T:(k + 1) * T],
                             w_switch_sb[:, k * EXPERTS:(k + 1) * EXPERTS],
                             start=(k == 0), stop=(k == KE - 1))
                ins.then_inc(logits_made, 1)

            def count(g, other=0):
                pe.wait_ge(route_steps, ROUTE_STEPS * g + 5)
                mm(route_banks[other][2], earlier, onehot[0:T, :], start=True, stop=True)
                mm(route_banks[other][3], ones_b, onehot[0:T, :], start=True, stop=True).then_inc(ranked, 1)

            def step(t, place):
                if runs(t, 0) and not (isinstance(t, int) and t == 1):
                    embed(t)
                if isinstance(t, int) and t == 0:
                    embed(1)
                    pe.wait_ge(embed_loaded, 16 * EMBED_LOADS)
                if isinstance(t, int) and t == 1:
                    pe.wait_ge(qk_loaded, 16 * QK_LOADS)
                alone = isinstance(t, int) and t == GROUPS
                if alone:
                    project_qk(t - 1)
                    project_v(t - 1)
                if runs(t, 2):
                    turn_probs(t - 2)
                if runs(t, 1) and not alone:
                    project_qk(t - 1)
                if isinstance(t, int) and t == 1:
                    pe.wait_ge(attn_loaded, 16 * ATTN_LOADS)
                    pe.wait_ge(dve_ready, 8)
                if runs(t, 2):
                    weigh(t - 2, 1 - place)
                if runs(t, 1) and not alone:
                    project_v(t - 1)
                if runs(t, 2):
                    turn_inverse(t - 2)
                early = isinstance(t, int) and t == 1
                if early:
                    keep_clock(WAIT_PRODUCTS)
                if runs(t, 0) and not early:
                    turn_normed(t)
                if runs(t, 4):
                    turn_normed2(t - 4, place, t - 4)
                if runs(t, 1):
                    score(t - 1, 0)
                if early:
                    turn_normed(t)
                if runs(t, 4):
                    route(t - 4)
                if runs(t, 2):
                    project_out(t - 2)
                if runs(t, 1):
                    score(t - 1, 1)
                if runs(t, 4):
                    count(t - 4)

            def finish():
                turn_probs(G)
                weigh(G, (G + 1) % 2)
                turn_inverse(G)
                turn_normed2(G - 2, 0, G - 2)
                route(G - 2, 0)
                project_out(G)
                count(G - 2, 0)
                turn_normed2(G - 1, 1, 0, other=1)
                route(G - 1, 1)
                turn_normed2(G, 0, G - 1)
                count(G - 1, 1)
                route(G, 0)
                count(G, 0)

            pe.wait_ge(dve_ready, 1)
            keep_clock(START_PRODUCTS)
            steps(pe, step, finish)

            pe.wait_ge(ffn_loaded, 16 * (WEIGHT_LOADS + 1))
            pe.wait_ge(tables_steps, TABLE_STEPS)
            keep_clock(FETCH_PRODUCTS)

            def turn_rows(b, r):
                pe.wait_ge(gathered[r], turns(b))
                if later(b):
                    pe.wait_ge(xT_made, b)
                for c in range(KE):
                    ins = turn(p_xT[:, c * P:(c + 1) * P], gathered_rows[r][:, EMBED + c * P:EMBED + (c + 1) * P],
                               ident[:, :])
                ins.then_inc(x_turned, 1)

            def block_step(b, r):
                if not later(b):
                    turn_rows(b + 1, (r + 1) % RING)
                if inside(b):
                    pe.wait_ge(xT_made, b + 1)
                    pe.wait_ge(w1_copied, b + 1)
                    for half in range(2):
                        if later(b, 2):
                            pe.wait_ge(gelu_made, 2 * (b - 2) + 1 + half)
                        for j in range(4):
                            at = (4 * half + j) * P
                            for k in range(KE):
                                ins = mm(p_hT[r % 2][half][:, j * P:(j + 1) * P],
                                         w1_now[r % 2][:, k * HIDDEN + at:k * HIDDEN + at + P],
                                         xT[r % 2][:, k * P:(k + 1) * P], start=(k == 0), stop=(k == KE - 1))
                        ins.then_inc(ffn_hidden, 1)
                if later(b) and inside(b + 1):
                    turn_rows(b + 1, (r + 1) % RING)
                if inside(b - 1):
                    e = pe.value_load(expert_of[0:1, ds(b - 1, 1)], min_val=0, max_val=EXPERTS - 1)
                    if later(b - 1, 2):
                        pe.wait_ge(ffn_read, b - 2)
                    for f in range(KH):
                        if f % 4 == 0:
                            pe.wait_ge(gelu_made, 2 * b - 1 + f // 4)
                        ins = mm(p_ffn[(r - 1) % 2][:, 0:EMBED], hT[(r - 1) % 2][:, f * P:(f + 1) * P],
                                 W[:, ds(W2_AT + e * KH * EMBED + f * EMBED, EMBED)],
                                 start=(f == 0), stop=(f == KH - 1))
                    ins.then_inc(ffn_done, 1)

            block_steps(pe, block_step)

        @block.vector
        def _(dve):
            v = nc.vector

            def settled():
                dve.sem_inc(dve_passed)

            def mean(i):
                return moments[0:T, 2 * i:2 * i + 1]

            def row_stats(i, rows, made, g, stats_sem):
                dve.wait_ge(made, g + 1)
                settled()
                v.bn_stats(stats[0:T, 6 * i:6 * i + 6], rows).then_inc(stats_sem, 1)

            def row_moments(i, g, stats_sem, moments_sem):
                dve.wait_ge(stats_sem, g + 1)
                settled()
                v.bn_aggr(moments[0:T, 2 * i:2 * i + 2], stats[0:T, 6 * i:6 * i + 6]).then_inc(moments_sem, 1)

            def embed_rows(g):
                dve.wait_ge(embedded, g + 1)
                v.tensor_tensor(hidden_of(g), p_h, position_sb[0:T, :], ALU.add) \
                    .then_inc(hidden_made, 1)

            def inverse_deviations(t):
                for stage, moments_sem in ((0, a_moments), (3, c_moments), (4, d_moments)):
                    if runs(t, stage):
                        dve.wait_ge(moments_sem, t - stage + 1)
                n = [RSTD_STEPS * t]

                def link(ins):
                    n[0] = n[0] + 1
                    ins.then_inc(rstd_steps, 1)
                    dve.wait_ge(rstd_steps, n[0])

                square, factor = newton[0:T, 0:3], newton[0:T, 3:6]
                x, y = var_eps[0:T, :], rstd[0:T, :]
                variance = moments[0:T, :].rearrange("p (i c) -> p i c", c=2)[:, :, 1]
                link(v.tensor_scalar(x, variance, EPS, None, ALU.add))
                link(v.tensor_scalar(square.bitcast(i32), x.bitcast(i32), 1, None, ALU.logical_shift_right))
                link(v.tensor_scalar(y.bitcast(i32), square.bitcast(i32), -1.0, float(0x5F3759DF),
                                     ALU.mult, ALU.add))
                for i in range(3):
                    v.tensor_tensor(square, y, y, ALU.mult).then_inc(rstd_steps, 1)
                    if i == 0 and runs(t, 3):
                        scale_attention(t - 3)
                    if i == 1 and runs(t, 2) and not (isinstance(t, int) and t > GROUPS):
                        widen_inverse(t - 2)
                    n[0] = n[0] + 1
                    dve.wait_ge(rstd_steps, n[0])
                    link(v.scalar_tensor_tensor(square, square, -0.5, x, ALU.mult, ALU.mult))
                    link(v.scalar_tensor_tensor(y, square, 1.5, y, ALU.add, ALU.mult))

            def normalize(g):
                if later(g):
                    dve.wait_ge(normed_turned, g)
                v.tensor_scalar(normed[0:T, :], hidden_of(g), mean(0), rstd[0:T, 0:1],
                                ALU.subtract, ALU.mult).then_inc(normed_made, 1)

            def normalize2(g, place):
                if later(g, 2):
                    dve.wait_ge(rows_written, 16 * (g - 1))
                v.tensor_scalar(payload[place][0:T, EMBED:2 * EMBED], hidden_of(g), mean(2),
                                rstd[0:T, 2:3], ALU.subtract, ALU.mult).then_inc(normed2_made, 1)

            def add_residual(g):
                dve.wait_ge(beta_added, g + 1)
                dve.wait_ge(attn_g_made, g + 1)
                h = hidden_of(g)
                v.scalar_tensor_tensor(h, attn_g[0:T, :], rstd[0:T, 1:2], h, ALU.mult, ALU.add) \
                    .then_inc(residual_made, 1)

            def find_top(g, half):
                if half == 0 and later(g):
                    dve.wait_ge(probs_made, 4 * g)
                dve.wait_ge(scored, 2 * g + half + 1)
                for r in (2 * half, 2 * half + 1):
                    v.tensor_reduce(top[0:T, 4 * r:4 * r + 4],
                                    scores[r][0:T, 0:4 * T].rearrange("p (j s) -> p j s", s=T),
                                    AX.X, ALU.max, negate=True).then_inc(top_found, 1)

            def copy_values(g, place):
                dve.wait_ge(v_made, g + 1)
                v.tensor_tensor(values[place][0:T, :].rearrange("p (h d) -> p h d", h=HEADS)[:, :, 0:HEAD],
                                p_v.rearrange("p (h d) -> p h d", h=HEADS),
                                bv.rearrange("p (h d) -> p h d", h=HEADS), ALU.add).then_inc(v_copied, 1)

            def invert(g):
                dve.wait_ge(probs_made, 4 * g + 4)
                if later(g):
                    dve.wait_ge(inverse_made, g)
                v.reciprocal(inverse[0:T, :], sums[0:T, :]).then_inc(inverted, 1)

            def widen_inverse(g):
                dve.wait_ge(inverted, g + 1)
                if later(g):
                    dve.wait_ge(inverse_turned, g)
                v.tensor_copy(inverse_wide[0:T, :].rearrange("p (h d) -> p h d", h=HEADS),
                              inverse[0:T, :].unsqueeze(2).broadcast_to([T, HEADS, HEAD])).then_inc(inverse_made, 1)

            def divide(g):
                dve.wait_ge(inverseT_made, g + 1)
                if later(g):
                    dve.wait_ge(projected, g)
                v.tensor_tensor(weightedT[:, :], p_oT, inverseT[:, :], ALU.mult).then_inc(weightedT_made, 1)

            def attention_rows(g):
                dve.wait_ge(projected, g + 1)
                v.tensor_tensor(attn[0:T, :], p_y, bo, ALU.add).then_inc(attn_made, 1)

            def scale_attention(g):
                dve.wait_ge(c_moments, g + 1)
                v.scalar_tensor_tensor(attn_g[0:T, :], attn[0:T, :], mean(1), gamma, ALU.subtract, ALU.mult) \
                    .then_inc(attn_g_made, 1)

            def pick(g, other=0):
                n = ROUTE_STEPS * g
                dve.wait_ge(logits_made, g + 1)
                if later(g):
                    dve.wait_ge(numer_made, g)
                v.scalar_tensor_tensor(negated[0:T, :], route_banks[other][1], -1.0, b_switch_sb[0:T, :],
                                       ALU.mult, ALU.subtract).then_inc(route_steps, 1)
                dve.wait_ge(route_steps, n + 1)
                v.tensor_reduce(best[0:T, 0:1], negated[0:T, :], AX.X, ALU.min).then_inc(route_steps, 1)
                dve.wait_ge(route_steps, n + 2)
                v.scalar_tensor_tensor(picks[0:T, :], negated[0:T, :], best[0:T, 0:1], col("descending", T),
                                       ALU.is_equal, ALU.mult).then_inc(route_steps, 1)
                dve.wait_ge(route_steps, n + 3)
                v.tensor_reduce(best[0:T, 1:2], picks[0:T, :], AX.X, ALU.max).then_inc(route_steps, 1)
                dve.wait_ge(route_steps, n + 4)
                if later(g):
                    dve.wait_ge(ranked, g)
                v.tensor_scalar(onehot[0:T, :], picks[0:T, :], best[0:T, 1:2], col("valid", T, g),
                                ALU.is_equal, ALU.mult).then_inc(route_steps, 1)

            def rank_rows(g, place, other=0):
                dve.wait_ge(numer_made, g + 1)
                v.reciprocal(payload[place][0:T, 2 * EMBED:2 * EMBED + 1], best[0:T, 2:3]).then_inc(prob_made, 1)
                dve.wait_ge(ranked, g + 1)
                if later(g):
                    dve.wait_ge(own_rank, 4 * g)
                v.tensor_tensor(rank[0:T, :], route_banks[other][2], next_slot[0:T, :], ALU.add) \
                    .then_inc(own_rank, 1)

            def keep_own_rank(g):
                dve.wait_ge(own_rank, 4 * g + 1)
                v.tensor_tensor(rank_own[0:T, :], rank[0:T, :], onehot[0:T, :], ALU.mult).then_inc(own_rank, 1)

            def set_slots(g, place, other=0):
                dve.wait_ge(own_rank, 4 * g + 2)
                v.tensor_reduce(slot_f[0:T, :], rank_own[0:T, :], AX.X, ALU.add).then_inc(own_rank, 1)
                v.tensor_tensor(next_slot[:, :], route_banks[other][3], next_slot[:, :], ALU.add) \
                    .then_inc(own_rank, 1)
                dve.wait_ge(own_rank, 4 * g + 3)
                if later(g, 2):
                    dve.wait_ge(ids_scattered, 16 * (g - 1))
                v.tensor_tensor(slot[0:T, place:place + 1], slot_f[0:T, :], col("trash_slot", T, g), ALU.add) \
                    .then_inc(route_steps, 1)

            def place_rows(g, place, other=0):
                rank_rows(g, place, other)
                keep_own_rank(g)
                set_slots(g, place, other)

            def a_row_moments(g):
                row_stats(0, hidden_of(g), hidden_made, g, a_stats)
                row_moments(0, g, a_stats, a_moments)

            def d_row_moments(g):
                row_stats(2, hidden_of(g), residual_made, g, d_stats)
                row_moments(2, g, d_stats, d_moments)

            def step(t, place):
                if runs(t, 0):
                    embed_rows(t)
                if runs(t, 2):
                    invert(t - 2)
                if runs(t, 0):
                    a_row_moments(t)
                if isinstance(t, int) and t == 1:
                    dve.wait_ge(qk_loaded, 16 * QK_LOADS)
                    v.tensor_copy(next_slot[:, :], col("first_slot")).then_inc(dve_ready, 1)
                    v.tensor_copy(masks_sb[0:T, :], big[0:T, 0:masks_sb.shape[1]]).then_inc(dve_ready, 1)
                    v.tensor_scalar(q_bias[:, :], b_qk_sb[:, 0:KE], SCALE, None, ALU.mult).then_inc(dve_ready, 1)
                    for parity, name in enumerate(("even", "odd")):
                        v.tensor_scalar(k_bias[:, KE * parity:KE * (parity + 1)], b_qk_sb[:, KE:2 * KE],
                                        col(name), None, ALU.mult).then_inc(dve_ready, 1)
                inverse_deviations(t)
                if runs(t, 0):
                    normalize(t)
                if runs(t, 4):
                    normalize2(t - 4, place)
                if runs(t, 1):
                    if isinstance(t, int) and t == 1:
                        dve.wait_ge(attn_loaded, 16 * ATTN_LOADS)
                    copy_values(t - 1, place)
                if runs(t, 3):
                    add_residual(t - 3)
                if runs(t, 2):
                    divide(t - 2)
                if runs(t, 3):
                    d_row_moments(t - 3)
                if runs(t, 1):
                    find_top(t - 1, 0)
                if runs(t, 4):
                    pick(t - 4)
                if runs(t, 2):
                    attention_rows(t - 2)
                if runs(t, 1):
                    find_top(t - 1, 1)
                if runs(t, 4):
                    rank_rows(t - 4, place)
                if runs(t, 2):
                    row_stats(1, attn[0:T, :], attn_made, t - 2, c_stats)
                if runs(t, 4):
                    keep_own_rank(t - 4)
                    set_slots(t - 4, place)
                if runs(t, 2):
                    row_moments(1, t - 2, c_stats, c_moments)

            v.memset(zeros[:, :], 0.0).then_inc(dve_ready, 1)
            v.memset(moments[:, :], 1.0)
            v.memset(values[0][:, :], 0.0)
            v.memset(values[1][:, :], 0.0).then_inc(dve_ready, 1)
            dve.wait_ge(dve_ready, 2)
            dve.wait_ge(embed_loaded, 16 * EMBED_LOADS)
            v.tensor_tensor(position_sb[0:T, :], position_sb[0:T, :], first_row_sb[0:T, :], ALU.add) \
                .then_inc(dve_ready, 1)
            dve.wait_ge(dve_ready, 3)
            def finish():
                invert(G)
                widen_inverse(G)
                inverse_deviations(GROUPS + 1)
                normalize2(G - 2, 0)
                divide(G)
                add_residual(G - 1)
                d_row_moments(G - 1)
                pick(G - 2, 0)
                attention_rows(G)
                rank_rows(G - 2, 0)
                row_stats(1, attn[0:T, :], attn_made, G, c_stats)
                keep_own_rank(G - 2)
                row_moments(1, G, c_stats, c_moments)
                set_slots(G - 2, 0)
                inverse_deviations(GROUPS + 2)
                add_residual(G)
                normalize2(G - 1, 1)
                d_row_moments(G)
                inverse_deviations(GROUPS + 3)
                normalize2(G, 0)
                pick(G - 1, 1)
                place_rows(G - 1, 1, 1)
                pick(G, 0)
                place_rows(G, 0, 0)

            steps(dve, step, finish)

            n = [0]

            def made(ins):
                n[0] += 1
                ins.then_inc(tables_steps, 1)

            def link(ins):
                made(ins)
                dve.wait_ge(tables_steps, n[0])

            def cube(ap, mid, last):
                return ap.rearrange("p (a b) -> p a b", b=last)

            def over(ap, mid, last):
                return ap.unsqueeze(2).broadcast_to([P, mid, last])

            def each_row(ap, mid, last):
                return ap.unsqueeze(1).broadcast_to([P, mid, last])

            E, B = EXPERTS, BLOCKS
            needs, ends, starts = (of_experts[:, i * E:(i + 1) * E] for i in range(3))
            base_and_last = of_experts[:, 3 * E:5 * E]
            own, source = of_blocks[:, 0:B], of_blocks[:, B:2 * B]
            of_own = of_blocks[:, 2 * B:4 * B]
            wide = scratch[:, 0:E * THRESH]
            dve.wait_ge(own_rank, 4 * GROUPS)
            link(v.tensor_tensor(cube(wide, E, THRESH), over(next_slot[:, :], E, THRESH),
                                 cube(col("threshold"), E, THRESH), ALU.is_gt))
            link(v.tensor_reduce(needs, cube(wide, E, THRESH), AX.X, ALU.add))
            square = scratch[:, 0:E * E]
            link(v.tensor_tensor(cube(square, E, E), each_row(needs, E, E), cube(col("upto"), E, E), ALU.mult))
            link(v.tensor_reduce(ends, cube(square, E, E), AX.X, ALU.add))
            below = scratch[:, 0:B * (E - 1)]
            made(v.tensor_tensor(cube(below, B, E - 1), each_row(ends[:, 0:E - 1], B, E - 1),
                                 over(col("block"), B, E - 1), ALU.is_le))
            made(v.tensor_tensor(starts, ends, needs, ALU.subtract))
            link(v.tensor_scalar(base_and_last[:, E:2 * E], next_slot[:, :], -1.0, None, ALU.add))
            made(v.tensor_reduce(own, cube(below, B, E - 1), AX.X, ALU.add))
            link(v.scalar_tensor_tensor(base_and_last[:, 0:E], starts, -float(P), col("region_row"),
                                        ALU.mult, ALU.add))
            made(v.tensor_tensor(cube(of_block[:, :], B, E), over(own, B, E), each_row(col("expert"), B, E),
                                 ALU.is_equal))
            link(v.tensor_copy(expert_of[:, :], own))
            picked = scratch[:, :]
            link(v.tensor_tensor(picked.rearrange("p (b i e) -> p b i e", i=2, e=E),
                                 cube(of_block[:, :], B, E).unsqueeze(2).broadcast_to([P, B, 2, E]),
                                 cube(base_and_last, 2, E).unsqueeze(1).broadcast_to([P, B, 2, E]), ALU.mult))
            link(v.tensor_reduce(of_own, cube(picked, 2 * B, E), AX.X, ALU.add))
            base_of, last_of = (cube(of_own, B, 2)[:, :, i] for i in range(2))
            link(v.tensor_tensor(source, base_of, col("block_row"), ALU.add))
            link(v.tensor_tensor(source_rows[:, :], source, last_of, ALU.min))
            link(v.tensor_tensor(live[:, :], source, last_of, ALU.is_le))
            assert n[0] == TABLE_STEPS

            def copy_w1(b, place):
                e = dve.value_load(expert_of[0:1, ds(b, 1)], min_val=0, max_val=EXPERTS - 1)
                if later(b, 2):
                    dve.wait_ge(ffn_hidden, 2 * b - 2)
                v.tensor_copy(w1_now[place][:, :], W[:, ds(e * KE * HIDDEN, KE * HIDDEN)]).then_inc(w1_copied, 1)

            dve.wait_ge(ffn_loaded, 16 * (WEIGHT_LOADS + 1))
            dve.wait_ge(projected, GROUPS)
            copy_w1(0, 0)
            dve.wait_ge(payload_copied, 2 * GROUPS)
            dve.wait_ge(normed2_made, GROUPS)
            copy_w1(1, 1)

            def block_step(b, r):
                if later(b, 0) and inside(b + 2):
                    copy_w1(b + 2, r % 2)
                if inside(b - 1):
                    q = (r - 1) % RING
                    rows = gathered_rows[q]
                    e = dve.value_load(expert_of[0:1, ds(b - 1, 1)], min_val=0, max_val=EXPERTS - 1)
                    dve.wait_ge(ffn_done, b)
                    if later(b - 1):
                        dve.wait_ge(result_made, b - 1)
                        dve.wait_ge(target_made, b - 1)
                    v.tensor_tensor(ffn_sum[:, :], p_ffn[q % 2][:, 0:EMBED], b2_sb[:, ds(e * EMBED, EMBED)], ALU.add) \
                        .then_inc(ffn_read, 1)
                    if later(b - 1, RING):
                        dve.wait_ge(stored, 16 * (b - RING))
                    v.scalar_tensor_tensor(target_f[:, :], rows[:, PAY - 1:PAY], col("trash_out"),
                                           live[:, ds(b - 1, 1)], ALU.subtract, ALU.mult).then_inc(target_diff, 1)
                    dve.wait_ge(target_diff, b)
                    v.tensor_tensor(target[:, q:q + 1], target_f[:, :], col("trash_out"), ALU.add) \
                        .then_inc(target_made, 1)
                    dve.wait_ge(ffn_read, b)
                    v.scalar_tensor_tensor(result[q], ffn_sum[:, :], rows[:, PAY - 2:PAY - 1], rows[:, 0:EMBED],
                                           ALU.mult, ALU.add).then_inc(result_made, 1)

            block_steps(dve, block_step)


def _constants():
    tab = np.zeros((P, TABLE_N), np.float32)
    row = np.arange(P)

    def put(name, value):
        a, b = TABLE[name]
        tab[:, a:b] = value

    put("even", (row % 32 < 16)[:, None])
    put("odd", (row % 32 >= 16)[:, None])
    put("trash_out", (ROWS + row)[:, None])
    put("region_row", REGION * np.arange(EXPERTS)[None, :] + row[:, None])
    put("block_row", P * np.arange(BLOCKS))
    put("descending", EXPERTS - np.arange(EXPERTS))
    put("first_slot", REGION * np.arange(EXPERTS))
    token = T * np.arange(GROUPS)[None, :] + row[:, None]
    put("valid", token < ROWS)
    put("trash_slot", (token >= ROWS) * (EXPERTS * REGION + row[:, None]))
    put("token", token)
    put("block", np.arange(BLOCKS))
    put("threshold", (REGION * np.arange(EXPERTS)[:, None] + P * np.arange(THRESH)).reshape(-1))
    e = np.arange(EXPERTS)
    put("upto", (e[None, :] <= e[:, None]).reshape(-1))
    put("expert", e)
    t = np.arange(T)
    seen = (t[:, None] // TOKENS == t[None, :] // TOKENS) & (t[None, :] <= t[:, None])
    masks = np.concatenate([np.tile(np.where(seen, 0.0, MASKED), (1, 4)), t[:, None] < t[None, :],
                            np.ones((T, P)), np.eye(T)], axis=1).astype(np.float32)
    return tab, np.eye(P, dtype=np.float32), masks


def kernel(**inputs):
    import concourse.bacc as _bacc
    from concourse.bass_utils import run_bass_kernel_spmd as _run

    x = {k: np.asarray(a) for k, a in inputs.items()}

    def rows_first(w, k):
        return w.reshape(k, P, -1).transpose(1, 0, 2).reshape(P, -1)

    def everywhere(v, parts=P):
        return np.broadcast_to(v.reshape(1, -1), (parts, v.size))

    img = x["x"].reshape(IMAGES, CHANNELS, GRID, PATCH, GRID, PATCH).transpose(1, 3, 5, 0, 2, 4)
    filled = np.zeros((PIXELS, GROUPS * PER, TOKENS), np.float32)
    filled[:, :IMAGES, 1:] = img.reshape(PIXELS, IMAGES, TOKENS - 1)
    patches = filled.reshape(KP, P, GROUPS, T).transpose(2, 1, 0, 3).reshape(GROUPS, P, KP * T)
    first = np.concatenate([x["L0_tok_cls_token"].reshape(1, EMBED),
                            everywhere(x["L0_tok_b"], TOKENS - 1)])
    w_qk = np.concatenate([x["L0_attn_Wq"], x["L0_attn_Wk"]], axis=1)
    b_qk = np.concatenate([x["L0_attn_bq"], x["L0_attn_bk"]]).reshape(4, P).T
    w1 = x["L0_ffn_w1"].reshape(EXPERTS, KE, P, HIDDEN).transpose(2, 0, 1, 3).reshape(P, -1)
    w2 = x["L0_ffn_w2"].reshape(EXPERTS, KH, P, EMBED).transpose(2, 0, 1, 3).reshape(P, -1)
    tab, eye, masks = _constants()
    arrays = {
        "patches": patches,
        "w_embed": rows_first(x["L0_tok_W"].T, KP),
        "position": np.tile(x["L0_tok_pos_embedding"].reshape(TOKENS, EMBED), (PER, 1)),
        "first_row": np.tile(first, (PER, 1)),
        "w_qk": rows_first(w_qk, KE), "b_qk": b_qk,
        "w_v": rows_first(x["L0_attn_Wv"], KE), "w_o": rows_first(x["L0_attn_Wo"], KE),
        "rows4": everywhere(np.concatenate([x["L0_attn_bv"], x["L0_attn_bo"], x["L0_attn_gamma"],
                                            x["L0_attn_beta"]])),
        "w_switch": rows_first(x["L0_ffn_switch_w"], KE), "b_switch": everywhere(x["L0_ffn_switch_b"]),
        "b1": x["L0_ffn_b1"].reshape(EXPERTS * KH, P).T, "b2": everywhere(x["L0_ffn_b2"]),
        "experts": np.concatenate([w1, w2], axis=1),
        "table": tab, "identity": eye, "masks": masks,
        "no_ids": np.zeros((EXPERTS * REGION + P, 1), np.int32),
    }
    nc = _bacc.Bacc("TRN2", target_bir_lowering=False, num_devices=1)
    arrays = {k: np.ascontiguousarray(a) for k, a in arrays.items()}
    args = [nc.dram_tensor(f"in_{k}_dram", a.shape, mybir.dt.from_np(a.dtype), kind="ExternalInput").ap()
            for k, a in arrays.items()]
    out = nc.dram_tensor("out_0_dram", (ROWS + P, EMBED), mybir.dt.float32, kind="ExternalOutput").ap()
    vit_layer(nc, *args, out)
    r = _run(nc, [{f"in_{k}_dram": a for k, a in arrays.items()}], core_ids=[0])
    return r.results[0]["out_0_dram"][:ROWS].reshape(IMAGES, TOKENS, EMBED)
```
